# Optimizing a Trainium2 kernel written in Bass

```python
import numpy as np
import jax
import jax.numpy as jnp

def _softmax(x, axis=-1):
    return jax.nn.softmax(x, axis=axis)

def _gelu(x):
    return jax.nn.gelu(x, approximate=True)

def _silu(x):
    return jax.nn.silu(x)

def _sigmoid(x):
    return jax.nn.sigmoid(x)

def _layernorm(x, axis=-1, eps=1e-05):
    m = jnp.mean(x, axis=axis, keepdims=True)
    v = jnp.var(x, axis=axis, keepdims=True)
    return (x - m) / jnp.sqrt(v + eps)

def _scatter_add(tgt, idx, src, axis=0):
    return tgt.at[idx].add(src)

def _segment_sum(src, seg, n):
    return jax.ops.segment_sum(src, seg, n)
kernel_name = 'mk_adj_resnorm_d2_adj_r2_1db261'

def setup_inputs(seed: int=0):
    np.random.seed(seed)
    _w = jnp.asarray

    def _rec_inputs():
        import jax
        import jax.numpy as jnp
        _gk = jax.random.key(seed)
        x = -9.806e-05 + 1 * jax.random.normal(jax.random.fold_in(_gk, 1), (4096, 64), jnp.float32)
        _a = jax.random.bernoulli(jax.random.fold_in(_gk, 2), 0.00390625, (4096, 4096))
        _a = jnp.logical_or(_a, jnp.swapaxes(_a, -1, -2))
        _a = jnp.logical_or(_a, jnp.eye(4096, dtype=bool))
        adj = _a.astype(jnp.int32)
        return (x, adj)
    x, adj = _rec_inputs()

    def _L0_gnn_setup():
        import jax, jax.numpy as jnp
        import numpy as np
        N = 4096
        F_IN = 64
        F_OUT = 64
        NEG_SLOPE = 0.01
        MASK_FILL = -1000000000000.0
        key = jax.random.key(seed)
        k1, k2, k3, k4 = jax.random.split(key, 4)
        x = jax.random.normal(k1, (N, F_IN), dtype=jnp.float32)
        adj_matrix = jax.random.randint(k2, (N, N), 0, 2, dtype=jnp.int32)
        W = jax.random.normal(k3, (F_IN, F_OUT), dtype=jnp.float32) * (1.0 / np.sqrt(F_IN))
        a = jax.random.normal(k4, (2 * F_IN, 1), dtype=jnp.float32) * (1.0 / np.sqrt(2 * F_IN))
        return {'x': x, 'adj_matrix': adj_matrix, 'W': W, 'a': a}
    _L0_gnn_all = _L0_gnn_setup()
    _L0_gnn_in = {k: v for k, v in _L0_gnn_all.items() if k in ('W', 'a')}
    del _L0_gnn_all

    def _L1_gnn_setup():
        import jax, jax.numpy as jnp
        import numpy as np
        N = 1024
        ATOM_D = 64
        H = 8
        NB = 8
        D = ATOM_D * H
        NEG_SLOPE = 0.2
        key = jax.random.key(seed)
        ks = jax.random.split(key, 12)
        inp = {'atom_embeddings': jax.random.normal(ks[0], (N, ATOM_D), dtype=jnp.float32), 'edges': jax.random.randint(ks[1], (N, N), -1, NB, dtype=jnp.int32), 'Qw': jax.random.normal(ks[2], (ATOM_D, D), dtype=jnp.float32) / np.sqrt(ATOM_D), 'Qb': jnp.zeros((D,), dtype=jnp.float32), 'Kw': jax.random.normal(ks[3], (ATOM_D, D), dtype=jnp.float32) / np.sqrt(ATOM_D), 'Kb': jnp.zeros((D,), dtype=jnp.float32), 'Vw': jax.random.normal(ks[4], (ATOM_D, D), dtype=jnp.float32) / np.sqrt(ATOM_D), 'Vb': jnp.zeros((D,), dtype=jnp.float32), 'a': jax.random.normal(ks[5], (NB, 2 * D, H), dtype=jnp.float32) * np.sqrt(2.0 / (2 * D + H)) * 1.414, 'Pw': jax.random.normal(ks[6], (D, ATOM_D), dtype=jnp.float32) / np.sqrt(D), 'Pb': jnp.zeros((ATOM_D,), dtype=jnp.float32)}
        return inp
    _L1_gnn_all = _L1_gnn_setup()
    _L1_gnn_in = {k: v for k, v in _L1_gnn_all.items() if k in ('Qw', 'Qb', 'Kw', 'Kb', 'Vw', 'Vb', 'a', 'Pw', 'Pb')}
    del _L1_gnn_all
    return {'x': x, 'adj': adj, 'L0_gnn_W': _L0_gnn_in['W'], 'L0_gnn_a': _L0_gnn_in['a'], 'L1_gnn_Qw': _L1_gnn_in['Qw'], 'L1_gnn_Qb': _L1_gnn_in['Qb'], 'L1_gnn_Kw': _L1_gnn_in['Kw'], 'L1_gnn_Kb': _L1_gnn_in['Kb'], 'L1_gnn_Vw': _L1_gnn_in['Vw'], 'L1_gnn_Vb': _L1_gnn_in['Vb'], 'L1_gnn_a': _L1_gnn_in['a'], 'L1_gnn_Pw': _L1_gnn_in['Pw'], 'L1_gnn_Pb': _L1_gnn_in['Pb']}

def reference(x, adj, L0_gnn_W, L0_gnn_a, L1_gnn_Qw, L1_gnn_Qb, L1_gnn_Kw, L1_gnn_Kb, L1_gnn_Vw, L1_gnn_Vb, L1_gnn_a, L1_gnn_Pw, L1_gnn_Pb):
    import jax
    import jax.numpy as jnp

    def _L0_gnn_ref(x, adj_matrix, W, a):
        import jax, jax.numpy as jnp
        import numpy as np
        N = 4096
        F_IN = 64
        F_OUT = 64
        NEG_SLOPE = 0.01
        MASK_FILL = -1000000000000.0
        h = x @ W
        a1 = a[:F_OUT, 0]
        a2 = a[F_OUT:, 0]
        f1 = h @ a1
        f2 = h @ a2
        e = jax.nn.leaky_relu(f1[:, None] + f2[None, :], NEG_SLOPE)
        e = jnp.where(adj_matrix > 0, e, MASK_FILL)
        attention = jax.nn.softmax(e, axis=1)
        h_prime = attention @ h
        return jax.nn.elu(h_prime)

    def _L1_gnn_ref(atom_embeddings, edges, Qw, Qb, Kw, Kb, Vw, Vb, a, Pw, Pb):
        import jax, jax.numpy as jnp
        import numpy as np
        N = 1024
        ATOM_D = 64
        H = 8
        NB = 8
        D = ATOM_D * H
        NEG_SLOPE = 0.2
        n, d = atom_embeddings.shape
        nb, two_d, h = a.shape
        D_ = two_d // 2
        Q = atom_embeddings @ Qw + Qb
        K = atom_embeddings @ Kw + Kb
        V = atom_embeddings @ Vw + Vb
        A1 = a[:, :D_, :]
        A2 = a[:, D_:, :]
        S1 = jnp.einsum('id,kdh->ikh', Q, A1)
        S2 = jnp.einsum('jd,kdh->jkh', K, A2)
        kidx = jnp.clip(edges, 0, nb - 1)
        rows = jnp.arange(n)
        e = S1[rows[:, None], kidx] + S2[rows[None, :], kidx]
        valid = (edges >= 0)[..., None]
        e = jnp.where(valid, jax.nn.leaky_relu(e, negative_slope=NEG_SLOPE), 0.0)
        attn = jax.nn.softmax(e, axis=1)
        Vh = V.reshape(n, h, d)
        out = jnp.einsum('ijh,jhd->ihd', attn, Vh).reshape(n, h * d)
        return out @ Pw + Pb
    x = _layernorm(x + _L0_gnn_ref(x, adj, L0_gnn_W, L0_gnn_a), axis=-1)
    x = _layernorm(x + _L1_gnn_ref(x, adj, L1_gnn_Qw, L1_gnn_Qb, L1_gnn_Kw, L1_gnn_Kb, L1_gnn_Vw, L1_gnn_Vb, L1_gnn_a, L1_gnn_Pw, L1_gnn_Pb), axis=-1)
    return x

_drawn_inputs = setup_inputs


def setup_inputs(seed=0):
    import zlib

    import numpy as np

    out = dict(_drawn_inputs(seed))
    spreads = {'L1_gnn_Qb': (0.0, 0.8),
     'L1_gnn_Kb': (0.0, 0.8),
     'L1_gnn_Vb': (0.0, 0.1),
     'L1_gnn_Pb': (0.0, 0.1)}
    factors = {}
    for name, (base, spread) in spreads.items():
        noise = np.random.default_rng([zlib.crc32(name.encode()), seed]).standard_normal(out[name].shape)
        drawn = base * np.exp(spread * noise) if base else spread * noise
        out[name] = jnp.asarray(drawn.astype(out[name].dtype))
    for name, factor in factors.items():
        out[name] = (out[name] * factor).astype(out[name].dtype)
    return out
```

```python
from contextlib import ExitStack

import concourse.bass as bass
from concourse import mybir

F32 = mybir.dt.float32
BF16 = mybir.dt.bfloat16
I8 = mybir.dt.int8
I32 = mybir.dt.int32
ALU = mybir.AluOpType
ACT = mybir.ActivationFunctionType
AX = mybir.AxisListType

P = 128
N = 4096
F = 64
NT = N // P
H = 8
TYPES = 8
KINDS = TYPES + 1
KH = KINDS * H
D1 = F * H
DC = D1 // P
SLOPE0 = 0.01
SLOPE1 = 0.2
EPS = 1e-5
LIMIT = 80.0

IB0 = 512
IT0 = IB0 // P
UNIT = 1024
UNITS = N // UNIT
HALF_J = 4
HALVES = 2 * UNITS
NB0 = N // IB0

IB1 = 1024
NB1 = N // IB1
PAIRS = H // 2
UNROLL = 4
STEPS = NT // UNROLL


class Shared:
    pass


def gat_program(nc, x, xT, adj, w0, w0T, a12, qwT, qb, kwT, kb, vwT, vb, a_cat, pw, pb, out):
    ctx = ExitStack()
    g = Shared()
    g.ctx = ctx
    g.x, g.xT, g.adj, g.w0, g.w0T, g.a12, g.out = x, xT, adj, w0, w0T, a12, out
    g.qwT, g.qb, g.kwT, g.kb, g.vwT, g.vb, g.a_cat, g.pw, g.pb = qwT, qb, kwT, kb, vwT, vb, a_cat, pw, pb

    def dram(name, shape, dt):
        return nc.dram_tensor(name, shape, dt).ap()

    g.codes_dram = dram("codes_t", (N, N), I8)
    g.r0_dram = dram("r0_row", (NT, P), F32)
    g.r_dram = dram("r_rows", (KH, N), F32)
    g.c_dram = dram("c_rows", (KH, N), F32)
    g.acc_dram = dram("acc_t", (NB1, P, PAIRS * IB1), F32)

    with ctx:
        def sb(name, shape, dt, stack=ctx):
            return stack.enter_context(nc.sbuf_tensor(name, shape, dt))

        def sem(name):
            return ctx.enter_context(nc.semaphore(name))

        g.sb, g.sem = sb, sem
        g.ident = sb("ident", [P, P], F32)
        g.ident_b = sb("ident_b", [P, P], BF16)
        g.ones = sb("ones", [P, P], F32)
        g.neg_kind = sb("neg_kind", [P, KINDS], F32)
        g.minus_half = sb("minus_half", [P, 1], F32)
        g.x_sb = sb("x_sb", [P, NT, F], F32)
        g.w0_ext = sb("w0_ext", [F + 1, F + 1], F32)
        g.g_fold = sb("g_fold", [F + 1, 2 * KH], F32)
        g.vp_fold = sb("vp_fold", [P, PAIRS, 2 * F + 2], F32)
        g.out_bias = sb("out_bias", [P, F], F32)
        g.hsum = sb("hsum", [P, F], F32)
        g.off_sum = sb("off_sum", [P, NB0 * UNITS], F32)
        g.num0 = sb("num0", [P, NT, F + 1], F32)
        g.x1 = sb("x1", [P, NT, F], F32)
        g.x1_one = sb("x1_one", [P, NT * F], F32)
        g.tau = sb("tau", [P, NT * KH], F32)
        g.w_exp = sb("w_exp", [P, NT * KH], F32)
        g.general = sb("general", [1, 1], I32)

        prepare(nc, g)
        layer0(nc, g)
        between(nc, g)
        layer1(nc, g)
        final(nc, g)


class Chain:

    def __init__(self, eng, semaphore):
        self.eng, self.semaphore, self.count = eng, semaphore, 0

    def __call__(self, instruction):
        self.count += 1
        instruction.then_inc(self.semaphore, 1)
        self.eng.wait_ge(self.semaphore, self.count)


def over_rows(ap, shape):
    return ap.unsqueeze(1).to_broadcast(shape)


def over_columns(ap, shape):
    return ap.unsqueeze(2).to_broadcast(shape)


def prepare(nc, g):
    sem, ctx = g.sem, g.ctx
    g.stack0 = ExitStack()
    g.tau0 = tau0 = g.sb("tau0", [P, NT], F32, g.stack0)
    g.x0_w = x0_w = g.sb("x0_w", [P, NT, F + 1], F32, g.stack0)
    g.r0_bc = r0_bc = g.sb("r0_bc", [P, N], F32, g.stack0)
    loaded = sem("small_inputs_loaded")
    consts = sem("consts_ready")
    dve_step = sem("prep_dve_step")
    pe_wa, wa_copied = sem("pe_wa"), sem("wa_copied")
    pe_f, f_copied = sem("pe_f"), sem("f_copied")
    pe_fold, pe_maxT, max_row = sem("pe_fold"), sem("pe_maxT"), sem("max_row")
    pe_beta, expo_ready, exps_done = sem("pe_beta"), sem("expo_ready"), sem("exps_done")
    pe_rT, r_copied, r_stored, r_bcast = sem("pe_rT"), sem("r_copied"), sem("r_stored"), sem("r_bcast")
    fold_in, pe_xsum, xsum_copied, pe_hsum = sem("fold_in"), sem("pe_xsum"), sem("xsum_copied"), sem("pe_hsum")
    LOADS = 14
    with ExitStack() as local:
        xT_sb = g.sb("xT_sb", [F, N], F32, local)
        w0T_sb = g.sb("w0T_sb", [F, F], F32, local)
        a12_sb = g.sb("a12_sb", [F, 2], F32, local)
        wa = g.sb("wa", [F, 2], F32, local)
        f12 = g.sb("f12", [P, NT, 2], F32, local)
        f2_max = g.sb("f2_max", [P, 1], F32, local)
        beta1 = g.sb("beta1", [1, 1], F32, local)
        beta = g.sb("beta", [P, 1], F32, local)
        expo = g.sb("expo", [P, 3, NT], F32, local)
        r0 = g.sb("r0", [P, NT], F32, local)
        w_0 = g.sb("w_0", [P, NT], F32, local)
        r0T = g.sb("r0T", [NT, P], F32, local)
        qk = g.sb("qk", [P, 2, DC, F + 1], F32, local)
        a_sb = g.sb("a_sb", [P, 2 * DC, TYPES * H], F32, local)
        vwT_sb = g.sb("vwT_sb", [F, H, F], F32, local)
        vwT_d = g.sb("vwT_d", [F, H, F], F32, local)
        vb_sb = g.sb("vb_sb", [F, H], F32, local)
        vb_bc = g.sb("vb_bc", [F, H, P], F32, local)
        pw_sb = g.sb("pw_sb", [F, H, F], F32, local)
        pb_sb = g.sb("pb_sb", [1, F], F32, local)
        xsum = g.sb("xsum", [F, P], F32, local)
        ps = [local.enter_context(nc.psum_tensor(f"prep_ps{i}", [P, 512], F32)) for i in range(8)]
        block = local.enter_context(nc.Block())

        @block.sync
        def _(sp):
            with nc.allow_non_contiguous_dma(reason="biases of one column"):
                for dst, src in (
                    (g.x_sb[:], g.x.rearrange("(t p) c -> p t c", p=P)),
                    (xT_sb[:], g.xT), (w0T_sb[:], g.w0T), (a12_sb[:], g.a12),
                    (g.w0_ext[0:F, 0:F], g.w0),
                    (qk[:, 0, :, 0:F], g.qwT.rearrange("(d p) c -> p d c", p=P)),
                    (qk[:, 1, :, 0:F], g.kwT.rearrange("(d p) c -> p d c", p=P)),
                    (qk[:, 0, :, F:F + 1], g.qb.rearrange("(d p o) -> p d o", p=P, o=1)),
                    (qk[:, 1, :, F:F + 1], g.kb.rearrange("(d p o) -> p d o", p=P, o=1)),
                    (a_sb[:], g.a_cat.rearrange("(d p) c -> p d c", p=P)),
                    (vwT_sb[:], g.vwT.rearrange("(h d) c -> d h c", d=F)),
                    (vb_sb[:], g.vb.rearrange("(h d) -> d h", d=F)),
                    (pw_sb[:], g.pw.rearrange("(h d) c -> d h c", d=F)),
                    (pb_sb[:], g.pb.rearrange("(o c) -> o c", o=1)),
                ):
                    sp.dma_start(dst, src).then_inc(loaded, 16)
            sp.wait_ge(r_copied, 1)
            sp.dma_start(g.r0_dram, r0T[:]).then_inc(r_stored, 16)
            sp.wait_ge(r_stored, 16)
            row = g.r0_dram.rearrange("t p -> (t p)").unsqueeze(0)
            sp.dma_start(r0_bc[:], row.to_broadcast([P, N])).then_inc(r_bcast, 16)
            sp.wait_ge(r_bcast, 16)

        @block.gpsimd
        def _(pool):
            pool.memset(g.ident[:], 0.0).then_inc(consts, 1)
            pool.memset(g.ident_b[:], 0.0).then_inc(consts, 1)
            pool.wait_ge(consts, 2)
            for m in (g.ident, g.ident_b):
                pool.affine_select(out=m[:], in_=m[:], compare_op=ALU.not_equal, fill=1.0, base=0,
                                   pattern=[[-1, P]], channel_multiplier=1).then_inc(consts, 1)
            pool.memset(g.ones[:], 1.0).then_inc(consts, 1)
            pool.memset(g.minus_half[:], -0.5).then_inc(consts, 1)
            for k in range(KINDS):
                code = k if k < TYPES else -1
                pool.memset(g.neg_kind[:, k:k + 1], float(-code)).then_inc(consts, 1)

        CONSTS = 6 + KINDS

        @block.vector
        def _(dve):
            step = Chain(dve, dve_step)
            step(nc.vector.memset(g.vp_fold[:], 0.0))
            step(nc.vector.memset(g.g_fold[:], 0.0))
            dve.wait_ge(loaded, 16 * LOADS)
            nc.vector.memset(g.w0_ext[0:F, F:F + 1], 0.0).then_inc(fold_in, 1)
            nc.vector.memset(g.w0_ext[F:F + 1, :], 0.0).then_inc(fold_in, 1)
            dve.wait_ge(fold_in, 2)
            nc.vector.memset(g.w0_ext[F:F + 1, F:F + 1], 1.0).then_inc(fold_in, 1)
            for h in range(H):
                nc.vector.tensor_scalar(vwT_d[:, h, :], vwT_sb[:, h, :], vwT_sb[:, h, F - 1:F], None,
                                        ALU.subtract).then_inc(fold_in, 1)
            dve.wait_ge(consts, CONSTS)
            nc.vector.tensor_tensor(vb_bc[:], over_columns(vb_sb[:], [F, H, P]),
                                    over_rows(g.ones[0:F, :], [F, H, P]), ALU.mult).then_inc(fold_in, 1)
            dve.wait_ge(pe_wa, 1)
            nc.vector.tensor_copy(wa[:], ps[0][0:F, 0:2]).then_inc(wa_copied, 1)
            dve.wait_ge(pe_f, 1)
            step(nc.vector.tensor_copy(f12[:].rearrange("p t c -> p (t c)"), ps[1][:, 0:2 * NT]))
            nc.vector.tensor_reduce(f2_max[:], f12[:, :, 1], AX.X, ALU.max).then_inc(f_copied, 1)
            dve.wait_ge(pe_maxT, 1)
            nc.vector.tensor_reduce(beta1[:], ps[5][0:1, 0:P], AX.X, ALU.max).then_inc(max_row, 1)
            dve.wait_ge(pe_beta, 1)
            step(nc.vector.tensor_copy(beta[:], ps[5][:, P:P + 1]))
            step(nc.vector.tensor_scalar(expo[:, 0, :], f12[:, :, 0], beta[:], 1.0 - SLOPE0, ALU.add, ALU.mult))
            step(nc.vector.tensor_scalar(expo[:, 0, :], expo[:, 0, :], LIMIT, None, ALU.min))
            step(nc.vector.tensor_scalar(expo[:, 2, :], f12[:, :, 1], beta[:], -LIMIT, ALU.subtract, ALU.max))
            nc.vector.tensor_scalar(expo[:, 1, :], expo[:, 2, :], -(1.0 - SLOPE0), None,
                                    ALU.mult).then_inc(expo_ready, 1)
            dve.wait_ge(pe_fold, 1)
            step(nc.vector.tensor_copy(g.g_fold[:, 0:TYPES * H], ps[2][0:F + 1, 0:TYPES * H]))
            step(nc.vector.tensor_copy(g.g_fold[:, KH:KH + TYPES * H], ps[2][0:F + 1, TYPES * H:2 * TYPES * H]))
            for s in range(2):
                rows = slice(s * F, (s + 1) * F)
                step(nc.vector.tensor_copy(g.vp_fold[rows, :, s * F:(s + 1) * F],
                                           ps[3][rows, 0:PAIRS * F].rearrange("p (q c) -> p q c", q=PAIRS)))
                step(nc.vector.tensor_copy(
                    g.vp_fold[rows, :, 2 * F + s:2 * F + s + 1],
                    over_rows(g.ident[rows, (s + 1) * F - 1:(s + 1) * F], [F, PAIRS, 1])))
            step(nc.vector.tensor_copy(g.out_bias[:], ps[4][:, 0:F]))
            dve.wait_ge(pe_xsum, 1)
            nc.vector.tensor_copy(xsum[:], ps[6][0:F, 0:P]).then_inc(xsum_copied, 1)
            dve.wait_ge(pe_hsum, 1)
            step(nc.vector.tensor_copy(g.hsum[:], ps[7][:, 0:F]))
            dve.wait_ge(exps_done, 3)
            step(nc.vector.tensor_tensor(x0_w[:, :, 0:F], g.x_sb[:], over_columns(w_0[:], [P, NT, F]), ALU.mult))
            step(nc.vector.tensor_copy(x0_w[:, :, F:F + 1], w_0[:].unsqueeze(2)))
            dve.wait_ge(pe_rT, 1)
            nc.vector.tensor_copy(r0T[:], ps[0][0:NT, 128:256]).then_inc(r_copied, 1)

        @block.scalar
        def _(act):
            act.wait_ge(expo_ready, 1)
            nc.scalar.activation(r0[:], expo[:, 0, :], ACT.Exp).then_inc(exps_done, 1)
            nc.scalar.activation(tau0[:], expo[:, 1, :], ACT.Exp).then_inc(exps_done, 1)
            nc.scalar.activation(w_0[:], expo[:, 2, :], ACT.Exp).then_inc(exps_done, 1)

        @block.tensor
        def _(pe):
            pe.wait_ge(loaded, 16 * LOADS)
            pe.wait_ge(consts, CONSTS)
            nc.tensor.matmul(ps[0][0:F, 0:2], w0T_sb[:], a12_sb[:], start=True, stop=True).then_inc(pe_wa, 1)
            pe.wait_ge(wa_copied, 1)
            for t in range(NT):
                last = nc.tensor.matmul(ps[1][:, 2 * t:2 * t + 2], xT_sb[:, t * P:(t + 1) * P], wa[:],
                                        start=True, stop=True)
            last.then_inc(pe_f, 1)
            for s in range(2):
                for d in range(DC):
                    nc.tensor.matmul(ps[2][0:F + 1, s * TYPES * H:(s + 1) * TYPES * H], qk[:, s, d, :],
                                     a_sb[:, s * DC + d, :], start=(d == 0), stop=(d == DC - 1))
            pe.wait_ge(fold_in, 3 + H + 1)
            for h in range(H):
                rows = slice((h % 2) * F, (h % 2 + 1) * F)
                nc.tensor.matmul(ps[3][rows, (h // 2) * F:(h // 2 + 1) * F], vwT_d[:, h, :], pw_sb[:, h, :],
                                 start=True, stop=True)
            nc.tensor.matmul(ps[4][:, 0:F], g.ones[0:1, :], pb_sb[:], start=True, stop=False)
            for h in range(H):
                last = nc.tensor.matmul(ps[4][:, 0:F], vb_bc[:, h, :], pw_sb[:, h, :], start=False,
                                        stop=(h == H - 1))
            last.then_inc(pe_fold, 1)
            pe.wait_ge(f_copied, 1)
            nc.tensor.transpose(ps[5][0:1, 0:P], f2_max[:], g.ident[:]).then_inc(pe_maxT, 1)
            pe.wait_ge(max_row, 1)
            nc.tensor.matmul(ps[5][:, P:P + 1], g.ones[0:1, :], beta1[:], start=True, stop=True).then_inc(pe_beta, 1)
            for t in range(NT):
                last = nc.tensor.matmul(ps[6][0:F, 0:P], g.x_sb[:, t, :], g.ones[:], start=(t == 0),
                                        stop=(t == NT - 1))
            last.then_inc(pe_xsum, 1)
            pe.wait_ge(xsum_copied, 1)
            nc.tensor.matmul(ps[7][:, 0:F], xsum[:], g.w0_ext[0:F, 0:F], start=True, stop=True).then_inc(pe_hsum, 1)
            pe.wait_ge(exps_done, 3)
            nc.tensor.transpose(ps[0][0:NT, 128:256], r0[:], g.ident[:]).then_inc(pe_rT, 1)


def layer0(nc, g):
    sem = g.sem
    raw_loaded = [sem(f"raw_loaded{u}") for u in range(UNITS)]
    code_ready = sem("code_ready")
    squared = sem("squared")
    transposed = sem("transposed")
    dense_ready = sem("dense_ready")
    t_ready = sem("t0_ready")
    multiplied = sem("multiplied")
    codes_out = sem("codes_out")
    codes_stored = [sem(f"codes_stored{n}") for n in range(2)]
    u_copied = sem("u_copied")
    num_ready, num_copied = sem("num_ready"), sem("num_copied")
    CREDIT = 4
    T_CREDIT = 2 * HALF_J
    with g.stack0, ExitStack() as local:
        raw = g.sb("raw", [P, UNITS, IT0, UNIT], I32, local)
        code = g.sb("code", [P, 2, IT0, UNIT], BF16, local)
        junk = g.sb("junk", [P, IT0 * UNIT], BF16, local)
        dense = g.sb("dense", [P, HALF_J, IB0], F32, local)
        t0 = g.sb("t0", [P, 2, HALF_J, IB0], F32, local)
        code_t = g.sb("code_t", [P, 2, HALF_J, IB0], I8, local)
        u_sb = g.sb("u_sb", [F + 1, IB0], F32, local)
        tp = local.enter_context(nc.psum_tensor("tp", [P, 2, HALF_J, IB0], BF16))
        u_ps = local.enter_context(nc.psum_tensor("u_ps", [P, IB0], F32))
        n_ps = local.enter_context(nc.psum_tensor("n_ps", [P, 512], F32))
        block = local.enter_context(nc.Block())

        @block.sync
        def _(sp):
            def load(b, u):
                rows = g.adj[bass.ds(b * IB0, IB0), u * UNIT:(u + 1) * UNIT]
                sp.dma_start(raw[:, u, :, :], rows.rearrange("(t p) j -> p t j", p=P)).then_inc(raw_loaded[u], 16)

            for u in range(UNITS):
                load(0, u)
            with sp.Fori(1, NB0) as b:
                for u in range(UNITS):
                    sp.wait_ge(code_ready, (b - 1) * UNITS + u + 1)
                    load(b, u)

        @block.vector
        def _(dve):
            dve.sem_inc(t_ready, T_CREDIT)
            with dve.Fori(0, NB0) as b:
                for u in range(UNITS):
                    unit = b * UNITS + u
                    dve.wait_ge(raw_loaded[u], 16 * b + 16)
                    dve.wait_ge(squared, unit + 1)
                    dve.wait_ge(transposed, 2 * unit + 2)
                    nc.vector.tensor_scalar(code[:, u % 2, :, :].rearrange("p t j -> p (t j)"),
                                            raw[:, u, :, :].rearrange("p t j -> p (t j)"), float(TYPES - 1), -1.0,
                                            ALU.min, ALU.max).then_inc(code_ready, 1)
                    for n in range(2):
                        half = unit * 2 + n
                        for a in range(HALF_J):
                            jt = (u * 2 + n) * HALF_J + a
                            dve.wait_ge(t_ready, half * HALF_J + (HALF_J + a + 1))
                            nc.vector.tensor_scalar(dense[:, a, :], r0_row(g, b), g.tau0[:, jt:jt + 1], None,
                                                    ALU.max).then_inc(dense_ready, 1)
                        dve.wait_ge(codes_out, half + 1)
                        dve.wait_ge(multiplied, half + 1)
                        for a in range(HALF_J):
                            dve.wait_ge(dense_ready, half * HALF_J + a + 1)
                            nc.vector.scalar_tensor_tensor(t0[:, n, a, :], code_t[:, n, a, :], 0.0, dense[:, a, :],
                                                           ALU.is_gt, ALU.mult).then_inc(t_ready, 1)

        @block.scalar
        def _(act):
            act.sem_inc(squared, 2)
            for n in range(2):
                act.sem_inc(codes_stored[n], 16)
            with act.Fori(0, NB0) as b:
                for u in range(UNITS):
                    unit = b * UNITS + u
                    act.wait_ge(code_ready, unit + 1)
                    nc.scalar.activation(junk[:], code[:, u % 2, :, :].rearrange("p t j -> p (t j)"), ACT.Square,
                                         bias=g.minus_half[:],
                                         accum_out=g.off_sum[:, bass.ds(unit, 1)]).then_inc(squared, 1)
                    for n in range(2):
                        half = unit * 2 + n
                        act.wait_ge(transposed, half + 1 + CREDIT)
                        act.wait_ge(codes_stored[n], 16 * unit + 16)
                        act.wait_ge(t_ready, half * HALF_J + HALF_J)
                        nc.scalar.activation(code_t[:, n, :, :].rearrange("p a i -> p (a i)"),
                                             tp[:, n, :, :].rearrange("p a i -> p (a i)"),
                                             ACT.Copy).then_inc(codes_out, 1)
                        act.wait_ge(codes_out, half + 1)
                        rows = (u * 2 + n) * HALF_J * P
                        dst = g.codes_dram[rows:rows + HALF_J * P, bass.ds(b * IB0, IB0)]
                        act.dma_start(dst.rearrange("(a p) i -> p a i", p=P),
                                      code_t[:, n, :, :]).then_inc(codes_stored[n], 16)
                act.wait_ge(multiplied, b * HALVES + HALVES + 2)
                nc.scalar.activation(u_sb[:], u_ps[0:F + 1, :], ACT.Copy).then_inc(u_copied, 1)
                act.wait_ge(num_ready, b + 1)
                nc.scalar.activation(
                    g.num0[:].rearrange("p t c -> p (t c)")[:, bass.ds(b * (IT0 * (F + 1)), IT0 * (F + 1))],
                    n_ps[:, 0:IT0 * (F + 1)], ACT.Copy).then_inc(num_copied, 1)
            for n in range(2):
                act.wait_ge(codes_stored[n], 16 * (NB0 * UNITS + 1))

        @block.tensor
        def _(pe):
            pe.sem_inc(transposed, CREDIT)
            pe.sem_inc(multiplied, 2)

            def transpose(b, u, n):
                half = (b * UNITS + u) * 2 + n
                if n == 0:
                    pe.wait_ge(code_ready, b * UNITS + u + 1)
                if half_known(half) is None or half >= 2:
                    pe.wait_ge(codes_out, half - 1)
                for a in range(HALF_J):
                    for t in range(IT0):
                        j = (n * HALF_J + a) * P
                        last = nc.tensor.transpose(tp[:, n, a, t * P:(t + 1) * P], code[:, u % 2, t, j:j + P],
                                                   g.ident_b[:])
                last.then_inc(transposed, 1)

            def multiply(b, u, n):
                half = (b * UNITS + u) * 2 + n
                if u == 0 and n == 0:
                    if half_known(b) is None or b >= 1:
                        pe.wait_ge(u_copied, b)
                for a in range(HALF_J):
                    jt = (u * 2 + n) * HALF_J + a
                    pe.wait_ge(t_ready, T_CREDIT + half * HALF_J + a + 1)
                    last = nc.tensor.matmul(u_ps[0:F + 1, :], g.x0_w[:, jt, :], t0[:, n, a, :], start=(jt == 0),
                                            stop=(jt == NT - 1))
                last.then_inc(multiplied, 1)

            order = [(u, n) for u in range(UNITS) for n in range(2)]

            def block_of_targets(b, last_block):
                for m, (u, n) in enumerate(order):
                    if m + 1 < HALVES:
                        transpose(b, *order[m + 1])
                    elif not last_block:
                        transpose(b + 1, 0, 0)
                    multiply(b, u, n)
                pe.wait_ge(u_copied, b + 1)
                if half_known(b) is None or b >= 1:
                    pe.wait_ge(num_copied, b)
                for t in range(IT0):
                    last = nc.tensor.matmul(n_ps[:, t * (F + 1):(t + 1) * (F + 1)], u_sb[:, t * P:(t + 1) * P],
                                            g.w0_ext[:], start=True, stop=True)
                last.then_inc(num_ready, 1)

            transpose(0, 0, 0)
            block_of_targets(0, False)
            with pe.Fori(1, NB0 - 1) as b:
                block_of_targets(b, False)
            block_of_targets(NB0 - 1, True)


def half_known(value):
    return value if isinstance(value, int) else None


def r0_row(g, b):
    return g.r0_bc[:, bass.ds(b * IB0, IB0)]


def between(nc, g):
    sem = g.sem
    dve_step = sem("between_dve_step")
    elu_in, elu_exp = sem("elu_in"), sem("elu_exp")
    centered, squares, var_ready, root = sem("centered0"), sem("squares0"), sem("var0"), sem("root0")
    x1_ready, xT_made, xT_copied = sem("x1_ready"), sem("x1T_made"), sem("x1T_copied")
    s_made, s_copied = sem("s_made"), sem("s_copied")
    max_ready, max_made, beta_diag, beta_made = sem("b_max"), sem("b_maxT"), sem("beta_diag"), sem("beta_made")
    expo_ready, exps_done = sem("expo1_ready"), sem("exps1_done")
    rows_made, rows_copied, rows_stored = sem("rows_made"), sem("rows_copied"), sem("rows_stored")
    flag_max, flag_T, flag_row = sem("flag_max"), sem("flag_T"), sem("flag_row")
    TG = 4
    SG = 3
    SGROUPS = -(-NT // SG)
    with ExitStack() as local:
        z = g.sb("z", [P, NT], F32, local)
        den = g.sb("den", [P, NT], F32, local)
        rec = g.sb("rec", [P, NT], F32, local)
        ha = g.sb("ha", [P, NT, F], F32, local)
        hb = g.sb("hb", [P, NT, F], F32, local)
        x1T = g.sb("x1T", [F + 1, N], F32, local)
        s12 = g.sb("s12", [P, NT, 2, KH], F32, local)
        b_max = g.sb("b_max", [P, KH], F32, local)
        beta_col = g.sb("beta_col", [KH, 1], F32, local)
        beta_d = g.sb("beta_d", [KH, KH], F32, local)
        beta_r = g.sb("beta_r", [P, KH], F32, local)
        e_r = g.sb("e_r", [P, NT, KH], F32, local)
        e_t = g.sb("e_t", [P, NT, KH], F32, local)
        e_c = g.sb("e_c", [P, NT, KH], F32, local)
        m_max = g.sb("m_max", [P, NT, H], F32, local)
        rowsT = g.sb("rowsT", [KH, 2, N], F32, local)
        off_max = g.sb("off_max", [P, 1], F32, local)
        off_row = g.sb("off_row", [1, 1], F32, local)
        absent = g.sb("absent", [P, 1], F32, local)
        ps = [local.enter_context(nc.psum_tensor(f"mid_ps{i}", [P, 512], F32)) for i in range(8)]
        block = local.enter_context(nc.Block())
        LOG = e_c

        @block.vector
        def _(dve):
            step = Chain(dve, dve_step)
            nc.vector.tensor_reduce(off_max[:], g.off_sum[:], AX.X, ALU.max).then_inc(flag_max, 1)
            step(nc.vector.tensor_scalar(z[:], g.num0[:, :, F], 0.0, None, ALU.is_equal))
            step(nc.vector.scalar_tensor_tensor(den[:], z[:], float(N), g.num0[:, :, F], ALU.mult, ALU.add))
            step(nc.vector.reciprocal(rec[:], den[:]))
            step(nc.vector.tensor_tensor(ha[:], over_rows(g.hsum[:], [P, NT, F]), over_columns(z[:], [P, NT, F]),
                                         ALU.mult))
            step(nc.vector.tensor_tensor(ha[:], ha[:], g.num0[:, :, 0:F], ALU.add))
            step(nc.vector.tensor_tensor(ha[:], ha[:], over_columns(rec[:], [P, NT, F]), ALU.mult))
            nc.vector.tensor_scalar(hb[:], ha[:], 0.0, None, ALU.min).then_inc(elu_in, 1)
            dve.wait_ge(flag_T, 1)
            step(nc.vector.tensor_reduce(off_row[:], ps[7][0:1, 0:P], AX.X, ALU.max))
            quiet = float(IT0 * UNIT) / 4.0
            step(nc.vector.tensor_scalar(off_row[:], off_row[:], quiet, None, ALU.is_gt))
            nc.vector.tensor_copy(g.general[:], off_row[:]).then_inc(flag_row, 1)
            dve.wait_ge(elu_exp, 1)
            step(nc.vector.scalar_tensor_tensor(ha[:], ha[:], 0.0, g.x_sb[:], ALU.max, ALU.add))
            step(nc.vector.scalar_tensor_tensor(ha[:], hb[:], -1.0, ha[:], ALU.add, ALU.add))
            step(nc.vector.tensor_reduce(z[:], ha[:], AX.X, ALU.add))
            step(nc.vector.tensor_scalar(z[:], z[:], 1.0 / F, None, ALU.mult))
            nc.vector.tensor_tensor(ha[:], ha[:], over_columns(z[:], [P, NT, F]), ALU.subtract).then_inc(centered, 1)
            dve.wait_ge(squares, 1)
            step(nc.vector.tensor_reduce(den[:], hb[:], AX.X, ALU.add))
            nc.vector.tensor_scalar(den[:], den[:], 1.0 / F, EPS, ALU.mult, ALU.add).then_inc(var_ready, 1)
            dve.wait_ge(root, 1)
            step(nc.vector.reciprocal(rec[:], rec[:]))
            step(nc.vector.tensor_tensor(g.x1[:], ha[:], over_columns(rec[:], [P, NT, F]), ALU.mult))
            step(nc.vector.memset(x1T[F:F + 1, :], 1.0))
            x1_one = g.x1_one[:].rearrange("p (t c) -> p t c", c=F)
            step(nc.vector.tensor_copy(x1_one[:, :, 0:F - 1], g.x1[:, :, 0:F - 1]))
            nc.vector.memset(x1_one[:, :, F - 1:F], 1.0).then_inc(x1_ready, 1)
            for n in range(NT // TG):
                dve.wait_ge(xT_made, n + 1)
                nc.vector.tensor_copy(x1T[0:F, n * TG * P:(n + 1) * TG * P], ps[n % 7][0:F, :]).then_inc(xT_copied, 1)
            for n in range(SGROUPS):
                m = min(SG, NT - n * SG)
                dve.wait_ge(s_made, n + 1)
                nc.vector.tensor_copy(s12[:, n * SG:n * SG + m, :, :].rearrange("p t s c -> p (t s c)"),
                                      ps[n % 7][:, 0:m * 2 * KH]).then_inc(s_copied, 1)
            dve.wait_ge(s_copied, SGROUPS)
            nc.vector.tensor_reduce(b_max[:], s12[:, :, 1, :].rearrange("p t c -> p c t"), AX.X,
                                    ALU.max).then_inc(max_ready, 1)
            dve.wait_ge(max_made, 1)
            step(nc.vector.tensor_reduce(beta_col[:], ps[7][0:KH, 0:P], AX.X, ALU.max))
            nc.vector.tensor_scalar(beta_d[:], g.ident[0:KH, 0:KH], beta_col[:], None, ALU.mult).then_inc(beta_diag, 1)
            dve.wait_ge(beta_made, 1)
            step(nc.vector.tensor_copy(beta_r[:], ps[7][:, P:P + KH]))
            wide = [P, NT, KH]
            step(nc.vector.tensor_tensor(e_t[:], s12[:, :, 1, :], over_rows(beta_r[:], wide), ALU.subtract))
            step(nc.vector.tensor_scalar(e_t[:], e_t[:], -LIMIT, None, ALU.max))
            step(nc.vector.tensor_tensor(e_r[:], s12[:, :, 0, :], over_rows(beta_r[:], wide), ALU.add))
            step(nc.vector.scalar_tensor_tensor(LOG[:], e_r[:], SLOPE1, e_r[:], ALU.mult, ALU.max))
            nc.vector.tensor_scalar(e_r[:], e_r[:], 1.0 - SLOPE1, LIMIT, ALU.mult, ALU.min).then_inc(expo_ready, 1)
            step(nc.vector.tensor_scalar(absent[:], ps[7][:, P + KH:P + KH + 1], -1.0, 1e30, ALU.add, ALU.mult))
            few = 2 * H
            step(nc.vector.tensor_scalar(s12[:, :, 0, few:KH], LOG[:, :, few:KH], absent[:], None, ALU.add))
            step(nc.vector.tensor_copy(s12[:, :, 0, 0:few], LOG[:, :, 0:few]))
            step(nc.vector.tensor_reduce(m_max[:], s12[:, :, 0, :].rearrange("p t (k h) -> p t h k", h=H), AX.X,
                                         ALU.max))
            dve.wait_ge(expo_ready, 1)
            for k in range(KINDS):
                cols = slice(k * H, (k + 1) * H)
                step(nc.vector.tensor_tensor(LOG[:, :, cols], LOG[:, :, cols], m_max[:], ALU.subtract))
            step(nc.vector.tensor_scalar(s12[:, :, 0, :], e_r[:], 0.0, None, ALU.max))
            step(nc.vector.tensor_tensor(LOG[:], LOG[:], s12[:, :, 0, :], ALU.subtract))
            nc.vector.tensor_scalar(LOG[:], LOG[:], 0.0, None, ALU.min).then_inc(expo_ready, 1)
            for n in range(2 * NT // TG):
                s, m = divmod(n, NT // TG)
                dve.wait_ge(rows_made, n + 1)
                nc.vector.tensor_copy(rowsT[:, s, m * TG * P:(m + 1) * TG * P],
                                      ps[n % 7][0:KH, :]).then_inc(rows_copied, 1)

        @block.scalar
        def _(act):
            act.wait_ge(elu_in, 1)
            nc.scalar.activation(hb[:], hb[:], ACT.Exp).then_inc(elu_exp, 1)
            act.wait_ge(centered, 1)
            nc.scalar.activation(hb[:], ha[:], ACT.Square).then_inc(squares, 1)
            act.wait_ge(var_ready, 1)
            nc.scalar.activation(rec[:], den[:], ACT.Sqrt).then_inc(root, 1)
            act.wait_ge(expo_ready, 1)
            tau_v = g.tau[:].rearrange("p (t c) -> p t c", c=KH)
            w_v = g.w_exp[:].rearrange("p (t c) -> p t c", c=KH)
            nc.scalar.activation(tau_v, e_t[:], ACT.Exp, scale=-(1.0 - SLOPE1)).then_inc(exps_done, 1)
            nc.scalar.activation(w_v, e_t[:], ACT.Exp).then_inc(exps_done, 1)
            act.wait_ge(expo_ready, 2)
            nc.scalar.activation(e_r[:], e_r[:], ACT.Exp).then_inc(exps_done, 1)
            nc.scalar.activation(e_c[:], e_c[:], ACT.Exp).then_inc(exps_done, 1)

        @block.tensor
        def _(pe):
            pe.wait_ge(flag_max, 1)
            nc.tensor.transpose(ps[7][0:1, 0:P], off_max[:], g.ident[:]).then_inc(flag_T, 1)
            pe.wait_ge(x1_ready, 1)
            for n in range(NT // TG):
                if n >= 7:
                    pe.wait_ge(xT_copied, n - 6)
                for t in range(TG):
                    last = nc.tensor.transpose(ps[n % 7][0:F, t * P:(t + 1) * P], g.x1[:, n * TG + t, :],
                                               g.ident[:])
                last.then_inc(xT_made, 1)
            for n in range(SGROUPS):
                m = min(SG, NT - n * SG)
                pe.wait_ge(xT_copied, NT // TG)
                if n >= 7:
                    pe.wait_ge(s_copied, n - 6)
                for t in range(m):
                    it = n * SG + t
                    last = nc.tensor.matmul(ps[n % 7][:, t * 2 * KH:(t + 1) * 2 * KH], x1T[:, it * P:(it + 1) * P],
                                            g.g_fold[:], start=True, stop=True)
                last.then_inc(s_made, 1)
            pe.wait_ge(max_ready, 1)
            nc.tensor.transpose(ps[7][0:KH, 0:P], b_max[:], g.ident[:]).then_inc(max_made, 1)
            pe.wait_ge(beta_diag, 1)
            nc.tensor.matmul(ps[7][:, P:P + KH], g.ones[0:KH, :], beta_d[:], start=True, stop=True)
            pe.wait_ge(flag_row, 1)
            nc.tensor.matmul(ps[7][:, P + KH:P + KH + 1], g.ones[0:1, :], off_row[:], start=True,
                             stop=True).then_inc(beta_made, 1)
            pe.wait_ge(exps_done, 4)
            for n in range(2 * NT // TG):
                s, m = divmod(n, NT // TG)
                if n >= 7:
                    pe.wait_ge(rows_copied, n - 6)
                for t in range(TG):
                    last = nc.tensor.transpose(ps[n % 7][0:KH, t * P:(t + 1) * P],
                                               (e_r, e_c)[s][:, m * TG + t, :], g.ident[:])
                last.then_inc(rows_made, 1)

        @block.sync
        def _(sp):
            for s, dst in enumerate((g.r_dram, g.c_dram)):
                sp.wait_ge(rows_copied, (s + 1) * (NT // TG))
                sp.dma_start(dst, rowsT[:, s, :]).then_inc(rows_stored, 16)
            sp.wait_ge(rows_stored, 32)


def layer1(nc, g):
    sem = g.sem
    codes_loaded = [sem(f"codes_loaded{n}") for n in range(UNROLL)]
    rows_loaded = [sem(f"rows_loaded{h}") for h in range(H)]
    factors_loaded = sem("factors_loaded")
    kind_set = sem("kind_set")
    mask_square = sem("mask_square")
    mask_ready = sem("mask_ready")
    w_ready = sem("w_ready")
    t_ready = sem("t1_ready")
    pairs_done = sem("pairs_done")
    u_copied = sem("u1_copied")
    weighed = sem("weighed")
    summed = sem("summed")
    acc_stored = sem("acc_stored")
    T_CREDIT = UNROLL * H
    P_CREDIT = UNROLL * PAIRS
    with ExitStack() as local:
        rows = g.sb("rows", [P, H, IB1], F32, local)
        factors = g.sb("factors", [P, PAIRS, IB1], F32, local)
        acc = g.sb("acc", [P, PAIRS, IB1], F32, local)
        u_sb = g.sb("u1_sb", [P, PAIRS, IB1], F32, local)
        t1 = g.sb("t1", [P, PAIRS, 2, IB1], F32, local)
        mask = g.sb("mask", [P, UNROLL, IB1], BF16, local)
        kind = g.sb("kind", [P, 1], F32, local)
        off_kind = g.sb("off_kind", [P, 2, IB1], BF16, local)
        codes = g.sb("codes", [P, UNROLL, IB1], I8, local)
        x_w = g.sb("x_w", [P, UNROLL, H, F], F32, local)
        u_ps = local.enter_context(nc.psum_tensor("u1_ps", [P, PAIRS, IB1], F32))
        block = local.enter_context(nc.Block())

        def either(eng, program):
            flag = eng.value_load(g.general[0:1, 0:1], min_val=0, max_val=1)
            with eng.If(flag != 0):
                program(KINDS)
            with eng.Else():
                program(2)

        def passes(eng, kinds, one_pass):
            with eng.Fori(0, NB1) as b:
                one_pass(b, 0, b * kinds)
                if kinds > 2:
                    with eng.Fori(1, kinds - 1) as k:
                        one_pass(b, k, b * kinds + k)
                one_pass(b, kinds - 1, b * kinds + (kinds - 1))

        @block.sync
        def _(sp):
            def program(kinds):
                def load_codes(b, s, number):
                    for n in range(UNROLL):
                        sp.wait_ge(mask_ready, number * UNROLL + n + 1)
                        src = g.codes_dram[bass.ds((s * UNROLL + n) * P, P), bass.ds(b * IB1, IB1)]
                        sp.dma_start(codes[:, n, :], src).then_inc(codes_loaded[n], 16)

                def one_pass(b, k, p):
                    for h in range(H):
                        sp.wait_ge(t_ready, p * (NT * H) + T_CREDIT - H + h + 1)
                        src = g.r_dram[bass.ds(k * H + h, 1), bass.ds(b * IB1, IB1)]
                        sp.dma_start(rows[:, h, :], src.to_broadcast([P, IB1])).then_inc(rows_loaded[h], 16)
                    with sp.Fori(1, 4) as s:
                        load_codes(b, s, p * STEPS + s)
                    sp.wait_ge(weighed, p + 1)
                    for q in range(PAIRS):
                        for s in range(2):
                            src = g.c_dram[bass.ds(k * H + 2 * q + s, 1), bass.ds(b * IB1, IB1)]
                            sp.dma_start(factors[s * F:(s + 1) * F, q, :],
                                         src.to_broadcast([F, IB1])).then_inc(factors_loaded, 16)
                    last_kind = isinstance(k, int) and k == kinds - 1
                    with sp.Fori(4, STEPS + 1) as s:
                        block_of_s = (b + s // STEPS) % NB1 if last_kind else b
                        load_codes(block_of_s, s % STEPS, p * STEPS + s)

                load_codes(0, 0, 0)
                passes(sp, kinds, one_pass)
                for n in range(UNROLL):
                    sp.wait_ge(codes_loaded[n], 16 * (NB1 * kinds * STEPS + 1))

            either(sp, program)

        @block.scalar
        def _(act):
            act.sem_inc(mask_ready, UNROLL)

            def program(kinds):
                def set_kind(k, number):
                    nc.scalar.activation(kind[:], g.neg_kind[:, bass.ds(k, 1)], ACT.Copy).then_inc(kind_set, 1)
                    act.wait_ge(kind_set, number + 1)

                def make_masks(number):
                    for n in range(UNROLL):
                        tile = number * UNROLL + n
                        act.wait_ge(codes_loaded[n], 16 * number + 16)
                        act.wait_ge(mask_ready, tile + (UNROLL - 1))
                        nc.scalar.activation(off_kind[:, n % 2, :], codes[:, n, :], ACT.Square,
                                             bias=kind[:]).then_inc(mask_square, 1)
                        act.wait_ge(mask_square, tile + 1)
                        act.wait_ge(t_ready, tile * H + H)
                        nc.scalar.activation(mask[:, n, :], off_kind[:, n % 2, :], ACT.Relu, bias=1.0,
                                             scale=-1.0).then_inc(mask_ready, 1)

                def one_pass(b, k, p):
                    with act.Fori(1, STEPS) as s:
                        make_masks(p * STEPS + s)
                    set_kind(0 if isinstance(k, int) and k == kinds - 1 else k + 1, p + 1)
                    make_masks((p + 1) * STEPS)
                    for q in range(PAIRS):
                        act.wait_ge(pairs_done, p * (NT * PAIRS) + (P_CREDIT + (NT - 1) * PAIRS + q + 1))
                        if q == 0:
                            act.wait_ge(summed, p + 1)
                        nc.scalar.activation(u_sb[:, q, :], u_ps[:, q, :], ACT.Copy).then_inc(u_copied, 1)

                set_kind(0, 0)
                make_masks(0)
                passes(act, kinds, one_pass)

            either(act, program)

        @block.gpsimd
        def _(pool):
            pool.sem_inc(weighed, 1)
            pool.sem_inc(summed, 1)

            def program(kinds):
                def one_pass(b, k, p):
                    with pool.Fori(0, STEPS) as s:
                        for n in range(UNROLL):
                            pool.wait_ge(pairs_done, (p * STEPS + s) * (UNROLL * PAIRS) + (n + 1) * PAIRS)
                            jt = s * UNROLL + n
                            wide = [P, H, F]
                            nc.gpsimd.tensor_tensor(
                                x_w[:, n, :, :], over_rows(g.x1_one[:, bass.ds(jt * F, F)], wide),
                                over_columns(g.w_exp[:, bass.ds(jt * KH + k * H, H)], wide),
                                ALU.mult).then_inc(w_ready, 1)
                    pool.wait_ge(factors_loaded, (p + 1) * (16 * H))
                    pool.wait_ge(u_copied, p * PAIRS + 2 * PAIRS)
                    if isinstance(k, int) and k == 0:
                        nc.gpsimd.tensor_tensor(acc[:], u_sb[:], factors[:], ALU.mult).then_inc(weighed, 1)
                        pool.wait_ge(weighed, p + 2)
                        pool.sem_inc(summed, 1)
                    else:
                        nc.gpsimd.tensor_tensor(u_sb[:], u_sb[:], factors[:], ALU.mult).then_inc(weighed, 1)
                        pool.wait_ge(weighed, p + 2)
                        nc.gpsimd.tensor_tensor(acc[:], acc[:], u_sb[:], ALU.add).then_inc(summed, 1)
                        pool.wait_ge(summed, p + 2)
                    if isinstance(k, int) and k == kinds - 1:
                        pool.dma_start(g.acc_dram[bass.ds(b, 1), :, :].rearrange("b p n -> (b p) n"),
                                       acc[:].rearrange("p q i -> p (q i)")).then_inc(acc_stored, 16)
                        pool.wait_ge(acc_stored, b * 16 + 16)

                passes(pool, kinds, one_pass)

            either(pool, program)

        @block.vector
        def _(dve):
            dve.sem_inc(t_ready, T_CREDIT)

            def program(kinds):
                def one_pass(b, k, p):
                    def step(s, first):
                        for n in range(UNROLL):
                            tile = p * NT + s * UNROLL + n
                            dve.wait_ge(mask_ready, tile + 1 + UNROLL)
                            for h in range(H):
                                q = h // 2
                                if h % 2 == 0:
                                    dve.wait_ge(pairs_done, tile * PAIRS + (P_CREDIT - PAIRS + q + 1))
                                if first and n == 0:
                                    dve.wait_ge(rows_loaded[h], 16 * p + 16)
                                col = (s * UNROLL + n) * KH + k * H + h
                                nc.vector.scalar_tensor_tensor(
                                    t1[:, q, h % 2, :], rows[:, h, :], g.tau[:, bass.ds(col, 1)], mask[:, n, :],
                                    ALU.max, ALU.mult).then_inc(t_ready, 1)

                    step(0, True)
                    with dve.Fori(1, STEPS) as s:
                        step(s, False)

                passes(dve, kinds, one_pass)

            either(dve, program)

        @block.tensor
        def _(pe):
            pe.sem_inc(pairs_done, P_CREDIT)
            pe.sem_inc(u_copied, PAIRS)

            def program(kinds):
                def multiply(tile, p, n, first, last_tile):
                    pe.wait_ge(w_ready, tile + 1)
                    for q in range(PAIRS):
                        pe.wait_ge(t_ready, tile * H + (T_CREDIT + 2 * q + 2))
                        if first:
                            pe.wait_ge(u_copied, p * PAIRS + q + 1)
                        for half in range(2):
                            cols = slice(half * 512, (half + 1) * 512)
                            for s in range(2):
                                last = nc.tensor.matmul(u_ps[s * F:(s + 1) * F, q, cols], x_w[:, n, 2 * q + s, :],
                                                        t1[:, q, s, cols], start=first, stop=last_tile)
                        last.then_inc(pairs_done, 1)

                def one_pass(b, k, p):
                    for n in range(UNROLL):
                        multiply(p * NT + n, p, n, n == 0, False)
                    with pe.Fori(1, STEPS - 1) as s:
                        for n in range(UNROLL):
                            multiply(p * NT + s * UNROLL + n, p, n, False, False)
                    for n in range(UNROLL):
                        multiply(p * NT + ((STEPS - 1) * UNROLL + n), p, n, False, n == UNROLL - 1)

                passes(pe, kinds, one_pass)

            either(pe, program)


def final(nc, g):
    sem = g.sem
    acc_loaded = [sem(f"acc_loaded{n}") for n in range(2)]
    projected, divided = sem("projected"), sem("divided")
    dve_step = sem("final_dve_step")
    centered, squares, var_ready, root = sem("centered1"), sem("squares1"), sem("var1"), sem("root1")
    out_ready, out_stored = sem("out_ready"), sem("out_stored")
    ITB = IB1 // P
    WIDE = 256
    with ExitStack() as local:
        acc = g.sb("acc_in", [P, 2, PAIRS, IB1], F32, local)
        rden = g.sb("rden", [P, 2, PAIRS, 2], F32, local)
        y = g.sb("y", [P, 2, H, F], F32, local)
        o = g.sb("o", [P, NT, F], F32, local)
        sq = g.sb("sq", [P, NT, F], F32, local)
        mean = g.sb("mean", [P, NT], F32, local)
        var = g.sb("var", [P, NT], F32, local)
        rec = g.sb("rec1", [P, NT], F32, local)
        ps = local.enter_context(nc.psum_tensor("fin_ps", [P, 2, PAIRS, WIDE], F32))
        block = local.enter_context(nc.Block())

        @block.sync
        def _(sp):
            for b in range(NB1):
                if b >= 2:
                    sp.wait_ge(projected, (b - 1) * ITB)
                sp.dma_start(acc[:, b % 2, :, :].rearrange("p q i -> p (q i)"),
                             g.acc_dram[b, :, :]).then_inc(acc_loaded[b % 2], 16)
            sp.wait_ge(out_ready, 1)
            sp.dma_start(g.out.rearrange("(t p) c -> p t c", p=P), o[:]).then_inc(out_stored, 16)
            sp.wait_ge(out_stored, 16)

        @block.tensor
        def _(pe):
            for it in range(NT):
                b, t = divmod(it, ITB)
                if t == 0:
                    pe.wait_ge(acc_loaded[b % 2], 16 * (b // 2 + 1))
                if it >= 2:
                    pe.wait_ge(divided, it - 1)
                for q in range(PAIRS):
                    last = nc.tensor.matmul(ps[:, it % 2, q, 0:2 * F + 2], acc[:, b % 2, q, t * P:(t + 1) * P],
                                            g.vp_fold[:, q, :], start=True, stop=True)
                last.then_inc(projected, 1)

        @block.vector
        def _(dve):
            step = Chain(dve, dve_step)
            for it in range(NT):
                n = it % 2
                dve.wait_ge(projected, it + 1)
                step(nc.vector.reciprocal(rden[:, n, :, :], ps[:, n, :, 2 * F:2 * F + 2]))
                heads = ps[:, n, :, 0:2 * F].rearrange("p q (s c) -> p q s c", s=2)
                rd = rden[:, n, :, :].unsqueeze(3).to_broadcast([P, PAIRS, 2, F])
                dve_out = y[:, n, :, :].rearrange("p (q s) c -> p q s c", s=2)
                nc.vector.tensor_tensor(dve_out, heads, rd, ALU.mult).then_inc(divided, 1)
                dve.wait_ge(divided, it + 1)
                step(nc.vector.tensor_reduce(o[:, it, :], y[:, n, :, :].rearrange("p h c -> p c h"), AX.X, ALU.add))
            step(nc.vector.tensor_tensor(o[:], o[:], g.x1[:], ALU.add))
            step(nc.vector.tensor_tensor(o[:], o[:], over_rows(g.out_bias[:], [P, NT, F]), ALU.add))
            step(nc.vector.tensor_reduce(mean[:], o[:], AX.X, ALU.add))
            step(nc.vector.tensor_scalar(mean[:], mean[:], 1.0 / F, None, ALU.mult))
            nc.vector.tensor_tensor(o[:], o[:], over_columns(mean[:], [P, NT, F]), ALU.subtract).then_inc(centered, 1)
            dve.wait_ge(squares, 1)
            step(nc.vector.tensor_reduce(var[:], sq[:], AX.X, ALU.add))
            nc.vector.tensor_scalar(var[:], var[:], 1.0 / F, EPS, ALU.mult, ALU.add).then_inc(var_ready, 1)
            dve.wait_ge(root, 1)
            step(nc.vector.reciprocal(rec[:], rec[:]))
            nc.vector.tensor_tensor(o[:], o[:], over_columns(rec[:], [P, NT, F]), ALU.mult).then_inc(out_ready, 1)

        @block.scalar
        def _(act):
            act.wait_ge(centered, 1)
            nc.scalar.activation(sq[:], o[:], ACT.Square).then_inc(squares, 1)
            act.wait_ge(var_ready, 1)
            nc.scalar.activation(rec[:], var[:], ACT.Sqrt).then_inc(root, 1)


def kernel(**inputs):
    import numpy as np
    import concourse.bacc as bacc
    from concourse.bass_utils import run_bass_kernel_spmd

    def laid(a):
        return np.ascontiguousarray(a)

    given = {name: np.asarray(a) for name, a in inputs.items()}
    x, adj, w0 = given["x"], given["adj"], given["L0_gnn_W"]
    arrays = {
        "x": laid(x), "xT": laid(x.T), "adj": laid(adj), "w0": laid(w0), "w0T": laid(w0.T),
        "a12": laid(given["L0_gnn_a"].reshape(2, F).T),
        "qwT": laid(given["L1_gnn_Qw"].T), "qb": laid(given["L1_gnn_Qb"]),
        "kwT": laid(given["L1_gnn_Kw"].T), "kb": laid(given["L1_gnn_Kb"]),
        "vwT": laid(given["L1_gnn_Vw"].T), "vb": laid(given["L1_gnn_Vb"]),
        "a_cat": laid(given["L1_gnn_a"].transpose(1, 0, 2).reshape(2 * D1, TYPES * H)),
        "pw": laid(given["L1_gnn_Pw"]), "pb": laid(given["L1_gnn_Pb"]),
    }
    nc = bacc.Bacc("TRN2", target_bir_lowering=False, num_devices=1)
    args = {name: nc.dram_tensor(f"in_{name}", a.shape, mybir.dt.from_np(a.dtype), kind="ExternalInput").ap()
            for name, a in arrays.items()}
    out = nc.dram_tensor("out_nodes", (N, F), F32, kind="ExternalOutput").ap()
    gat_program(nc, out=out, **args)
    result = run_bass_kernel_spmd(nc, [{f"in_{name}": a for name, a in arrays.items()}], core_ids=[0])
    return result.results[0]["out_nodes"]
```

```python
from contextlib import ExitStack

import concourse.bass as bass
from concourse import mybir

F32 = mybir.dt.float32
BF16 = mybir.dt.bfloat16
I8 = mybir.dt.int8
I32 = mybir.dt.int32
ALU = mybir.AluOpType
ACT = mybir.ActivationFunctionType
AX = mybir.AxisListType

P = 128
N = 4096
F = 64
NT = N // P
H = 8
TYPES = 8
KINDS = TYPES + 1
KH = KINDS * H
D1 = F * H
DC = D1 // P
SLOPE0 = 0.01
SLOPE1 = 0.2
EPS = 1e-5
LIMIT = 80.0

IB0 = 1024
IT0 = IB0 // P
UNIT = 512
UNITS = N // UNIT
HALF_J = 2
HALVES = 2 * UNITS
NB0 = N // IB0
RAW = 4
BANK = 512

IB1 = 2048
NB1 = N // IB1
HG = 4
GROUPS = H // HG
VISITS = NB1 * GROUPS
PAIRS = HG // 2
UNROLL = 4
STEPS = NT // UNROLL


class Shared:
    pass


def gat_program(nc, x, xT, adj, w0, w0T, a12, qwT, qb, kwT, kb, vwT, vb, a_cat, pw, pb, out):
    ctx = ExitStack()
    g = Shared()
    g.ctx = ctx
    g.x, g.xT, g.adj, g.w0, g.w0T, g.a12, g.out = x, xT, adj, w0, w0T, a12, out
    g.qwT, g.qb, g.kwT, g.kb, g.vwT, g.vb, g.a_cat, g.pw, g.pb = qwT, qb, kwT, kb, vwT, vb, a_cat, pw, pb

    def dram(name, shape, dt):
        return nc.dram_tensor(name, shape, dt).ap()

    g.codes_dram = dram("codes_t", (N, N), I8)
    g.r0_dram = dram("r0_row", (NT, P), F32)
    g.r_dram = dram("r_rows", (KH, N), F32)
    g.c_dram = dram("c_rows", (KH, N), F32)
    g.acc_dram = dram("acc_t", (VISITS * KINDS, P, PAIRS, IB1), F32)

    with ctx:
        def sb(name, shape, dt, stack=ctx):
            return stack.enter_context(nc.sbuf_tensor(name, shape, dt))

        def sem(name):
            return ctx.enter_context(nc.semaphore(name))

        g.sb, g.sem = sb, sem
        g.ident = sb("ident", [P, P], F32)
        g.ident_b = sb("ident_b", [P, P], BF16)
        g.ones = sb("ones", [P, P], F32)
        g.neg_kind = sb("neg_kind", [P, KINDS], F32)
        g.minus_half = sb("minus_half", [P, 1], F32)
        g.g_fold = sb("g_fold", [F + 1, 2 * KH], F32)
        g.vp_fold = sb("vp_fold", [P, H // 2, 2 * F + 2], F32)
        g.out_bias = sb("out_bias", [P, F], F32)
        g.x1 = sb("x1", [P, NT, F], F32)
        g.x1_one = sb("x1_one", [P, NT * F], F32)
        g.tau = sb("tau", [P, NT * KH], F32)
        g.w_exp = sb("w_exp", [P, NT * KH], F32)
        g.general = sb("general", [1, 1], I32)

        with ExitStack() as early:
            g.x_sb = sb("x_sb", [P, NT, F], F32, early)
            g.num0 = sb("num0", [P, NT, F + 1], F32, early)
            g.hsum = sb("hsum", [P, F], F32, early)
            g.off_sum = sb("off_sum", [P, NB0 * UNITS], F32, early)
            with ExitStack() as first:
                g.w0_twice = sb("w0_twice", [P, F], F32, first)
                g.den_rows = sb("den_rows", [P, 1], F32, first)
                g.tau0 = sb("tau0", [P, NT], F32, first)
                g.x0_w = sb("x0_w", [P, NT, F], F32, first)
                g.w0_rep = sb("w0_rep", [P, NT, 32], F32, first)
                g.r0_bc = sb("r0_bc", [P, N], F32, first)
                g.raw = sb("raw", [P, RAW, IT0, UNIT], I32, first)
                g.raw_loaded = [sem(f"raw_loaded{n}") for n in range(RAW)]
                prepare(nc, g)
                layer0(nc, g)
            between(nc, g)
        layer1(nc, g)
        final(nc, g)


class Chain:

    def __init__(self, eng, semaphore):
        self.eng, self.semaphore, self.count = eng, semaphore, 0

    def __call__(self, instruction):
        self.count += 1
        instruction.then_inc(self.semaphore, 1)
        self.eng.wait_ge(self.semaphore, self.count)


def over_rows(ap, shape):
    return ap.unsqueeze(1).to_broadcast(shape)


def over_columns(ap, shape):
    return ap.unsqueeze(2).to_broadcast(shape)


def load_adj(sp, g, b, u):
    rows = g.adj[bass.ds(b * IB0, IB0), u * UNIT:(u + 1) * UNIT]
    sp.dma_start(g.raw[:, u % RAW, :, :], rows.rearrange("(t p) j -> p t j", p=P)).then_inc(g.raw_loaded[u % RAW], 16)


def either(eng, g, program):
    flag = eng.value_load(g.general[0:1, 0:1], min_val=0, max_val=1)
    with eng.If(flag != 0):
        program(KINDS)
    with eng.Else():
        program(2)


def prepare(nc, g):
    sem = g.sem
    tau0, x0_w, r0_bc = g.tau0, g.x0_w, g.r0_bc
    loaded, w_loaded = sem("inputs_loaded"), sem("weights_loaded")
    consts = sem("consts_ready")
    dve_step = sem("prep_dve_step")
    pe_wa, wa_copied = sem("pe_wa"), sem("wa_copied")
    pe_f, f_copied = sem("pe_f"), sem("f_copied")
    pe_fold, pe_maxT, max_row = sem("pe_fold"), sem("pe_maxT"), sem("max_row")
    pe_beta, expo_ready, exps_done = sem("pe_beta"), sem("expo_ready"), sem("exps_done")
    pe_rT, r_copied, r_stored, r_bcast = sem("pe_rT"), sem("r_copied"), sem("r_stored"), sem("r_bcast")
    fold_in, pe_xsum, xsum_copied, pe_hsum = sem("fold_in"), sem("pe_xsum"), sem("xsum_copied"), sem("pe_hsum")
    NP = H // 2
    with ExitStack() as local:
        xT_sb = g.sb("xT_sb", [F, N], F32, local)
        w0T_sb = g.sb("w0T_sb", [F, F], F32, local)
        a12_sb = g.sb("a12_sb", [F, 2], F32, local)
        wa = g.sb("wa", [F, 2], F32, local)
        f12 = g.sb("f12", [P, NT, 2], F32, local)
        f2_max = g.sb("f2_max", [P, 1], F32, local)
        beta1 = g.sb("beta1", [1, 1], F32, local)
        beta = g.sb("beta", [P, 1], F32, local)
        expo = g.sb("expo", [P, 3, NT], F32, local)
        r0 = g.sb("r0", [P, NT], F32, local)
        w_0 = g.sb("w_0", [P, NT], F32, local)
        r0T = g.sb("r0T", [NT, P], F32, local)
        qk = g.sb("qk", [P, 2, DC, F + 1], F32, local)
        a_sb = g.sb("a_sb", [P, 2 * DC, TYPES * H], F32, local)
        vwT_sb = g.sb("vwT_sb", [F, H, F], F32, local)
        vwT_d = g.sb("vwT_d", [F, H, F], F32, local)
        vb_sb = g.sb("vb_sb", [F, H], F32, local)
        vb_bc = g.sb("vb_bc", [F, H, P], F32, local)
        pw_sb = g.sb("pw_sb", [F, H, F], F32, local)
        pb_sb = g.sb("pb_sb", [1, F], F32, local)
        xsum = g.sb("xsum", [F, P], F32, local)
        ps = [local.enter_context(nc.psum_tensor(f"prep_ps{i}", [P, BANK], F32)) for i in range(8)]
        block = local.enter_context(nc.Block())
        first_inputs = ((w0T_sb[:], g.w0T), (a12_sb[:], g.a12), (xT_sb[:], g.xT),
                        (g.x_sb[:], g.x.rearrange("(t p) c -> p t c", p=P)),
                        (g.w0_twice[0:F, :], g.w0), (g.w0_twice[F:2 * F, :], g.w0))
        weights = ((qk[:, 0, :, 0:F], g.qwT.rearrange("(d p) c -> p d c", p=P)),
                   (qk[:, 1, :, 0:F], g.kwT.rearrange("(d p) c -> p d c", p=P)),
                   (qk[:, 0, :, F:F + 1], g.qb.rearrange("(d p o) -> p d o", p=P, o=1)),
                   (qk[:, 1, :, F:F + 1], g.kb.rearrange("(d p o) -> p d o", p=P, o=1)),
                   (a_sb[:], g.a_cat.rearrange("(d p) c -> p d c", p=P)),
                   (vwT_sb[:], g.vwT.rearrange("(h d) c -> d h c", d=F)),
                   (vb_sb[:], g.vb.rearrange("(h d) -> d h", d=F)),
                   (pw_sb[:], g.pw.rearrange("(h d) c -> d h c", d=F)),
                   (pb_sb[:], g.pb.rearrange("(o c) -> o c", o=1)))

        @block.sync
        def _(sp):
            for dst, src in first_inputs:
                sp.dma_start(dst, src).then_inc(loaded, 16)
            for u in range(RAW):
                load_adj(sp, g, 0, u)
            sp.wait_ge(r_copied, 1)
            sp.dma_start(g.r0_dram, r0T[:]).then_inc(r_stored, 16)
            sp.wait_ge(r_stored, 16)
            row = g.r0_dram.rearrange("t p -> (t p)").unsqueeze(0)
            sp.dma_start(r0_bc[:], row.to_broadcast([P, N])).then_inc(r_bcast, 16)
            sp.wait_ge(r_bcast, 16)

        @block.gpsimd
        def _(pool):
            pool.memset(g.ident[:], 0.0).then_inc(consts, 1)
            pool.memset(g.ident_b[:], 0.0).then_inc(consts, 1)
            pool.wait_ge(consts, 2)
            for m in (g.ident, g.ident_b):
                pool.affine_select(out=m[:], in_=m[:], compare_op=ALU.not_equal, fill=1.0, base=0,
                                   pattern=[[-1, P]], channel_multiplier=1).then_inc(consts, 1)
            pool.memset(g.ones[:], 1.0).then_inc(consts, 1)
            pool.memset(g.minus_half[:], -0.5).then_inc(consts, 1)
            for k in range(KINDS):
                code = k if k < TYPES else -1
                pool.memset(g.neg_kind[:, k:k + 1], float(-code)).then_inc(consts, 1)

        CONSTS = 6 + KINDS

        @block.scalar
        def _(act):
            with nc.allow_non_contiguous_dma(reason="biases of one column"):
                for dst, src in weights:
                    act.dma_start(dst, src).then_inc(w_loaded, 16)
            act.wait_ge(expo_ready, 1)
            nc.scalar.activation(r0[:], expo[:, 0, :], ACT.Exp).then_inc(exps_done, 1)
            nc.scalar.activation(tau0[:], expo[:, 1, :], ACT.Exp).then_inc(exps_done, 1)
            nc.scalar.activation(w_0[:], expo[:, 2, :], ACT.Exp).then_inc(exps_done, 1)

        @block.vector
        def _(dve):
            step = Chain(dve, dve_step)
            step(nc.vector.memset(g.vp_fold[:], 0.0))
            step(nc.vector.memset(g.g_fold[:], 0.0))
            dve.wait_ge(pe_wa, 1)
            nc.vector.tensor_copy(wa[:], ps[0][0:F, 0:2]).then_inc(wa_copied, 1)
            dve.wait_ge(pe_f, 1)
            step(nc.vector.tensor_copy(f12[:].rearrange("p t c -> p (t c)"), ps[1][:, 0:2 * NT]))
            nc.vector.tensor_reduce(f2_max[:], f12[:, :, 1], AX.X, ALU.max).then_inc(f_copied, 1)
            dve.wait_ge(pe_maxT, 1)
            nc.vector.tensor_reduce(beta1[:], ps[5][0:1, 0:P], AX.X, ALU.max).then_inc(max_row, 1)
            dve.wait_ge(pe_beta, 1)
            step(nc.vector.tensor_copy(beta[:], ps[5][:, P:P + 1]))
            step(nc.vector.tensor_scalar(expo[:, 0, :], f12[:, :, 0], beta[:], 1.0 - SLOPE0, ALU.add, ALU.mult))
            step(nc.vector.tensor_scalar(expo[:, 0, :], expo[:, 0, :], LIMIT, None, ALU.min))
            step(nc.vector.tensor_scalar(expo[:, 2, :], f12[:, :, 1], beta[:], -LIMIT, ALU.subtract, ALU.max))
            nc.vector.tensor_scalar(expo[:, 1, :], expo[:, 2, :], -(1.0 - SLOPE0), None,
                                    ALU.mult).then_inc(expo_ready, 1)
            dve.wait_ge(pe_rT, 1)
            nc.vector.tensor_copy(r0T[:], ps[0][0:NT, 128:256]).then_inc(r_copied, 1)
            dve.wait_ge(exps_done, 3)
            dve.wait_ge(loaded, 16 * len(first_inputs))
            step(nc.vector.tensor_tensor(x0_w[:], g.x_sb[:], over_columns(w_0[:], [P, NT, F]), ALU.mult))
            step(nc.vector.tensor_copy(g.w0_rep[:], over_columns(w_0[:], [P, NT, 32])))
            dve.wait_ge(consts, CONSTS)
            step(nc.vector.tensor_reduce(g.den_rows[:], g.ident[:, 0:P:32], AX.X, ALU.add))
            dve.wait_ge(w_loaded, 16 * len(weights))
            for h in range(H):
                nc.vector.tensor_scalar(vwT_d[:, h, :], vwT_sb[:, h, :], vwT_sb[:, h, F - 1:F], None,
                                        ALU.subtract).then_inc(fold_in, 1)
            nc.vector.tensor_tensor(vb_bc[:], over_columns(vb_sb[:], [F, H, P]),
                                    over_rows(g.ones[0:F, :], [F, H, P]), ALU.mult).then_inc(fold_in, 1)
            dve.wait_ge(pe_xsum, 1)
            nc.vector.tensor_copy(xsum[:], ps[6][0:F, 0:P]).then_inc(xsum_copied, 1)
            dve.wait_ge(pe_hsum, 1)
            step(nc.vector.tensor_copy(g.hsum[:], ps[7][:, 0:F]))
            dve.wait_ge(pe_fold, 1)
            step(nc.vector.tensor_copy(g.g_fold[:, 0:TYPES * H], ps[2][0:F + 1, 0:TYPES * H]))
            step(nc.vector.tensor_copy(g.g_fold[:, KH:KH + TYPES * H], ps[2][0:F + 1, TYPES * H:2 * TYPES * H]))
            for s in range(2):
                rows = slice(s * F, (s + 1) * F)
                step(nc.vector.tensor_copy(g.vp_fold[rows, :, s * F:(s + 1) * F],
                                           ps[3][rows, 0:NP * F].rearrange("p (q c) -> p q c", q=NP)))
                step(nc.vector.tensor_copy(
                    g.vp_fold[rows, :, 2 * F + s:2 * F + s + 1],
                    over_rows(g.ident[rows, (s + 1) * F - 1:(s + 1) * F], [F, NP, 1])))
            step(nc.vector.tensor_copy(g.out_bias[:], ps[4][:, 0:F]))

        @block.tensor
        def _(pe):
            pe.wait_ge(loaded, 16 * len(first_inputs))
            nc.tensor.matmul(ps[0][0:F, 0:2], w0T_sb[:], a12_sb[:], start=True, stop=True).then_inc(pe_wa, 1)
            pe.wait_ge(wa_copied, 1)
            for t in range(NT):
                last = nc.tensor.matmul(ps[1][:, 2 * t:2 * t + 2], xT_sb[:, t * P:(t + 1) * P], wa[:],
                                        start=True, stop=True)
            last.then_inc(pe_f, 1)
            pe.wait_ge(consts, CONSTS)
            pe.wait_ge(f_copied, 1)
            nc.tensor.transpose(ps[5][0:1, 0:P], f2_max[:], g.ident[:]).then_inc(pe_maxT, 1)
            pe.wait_ge(max_row, 1)
            nc.tensor.matmul(ps[5][:, P:P + 1], g.ones[0:1, :], beta1[:], start=True, stop=True).then_inc(pe_beta, 1)
            pe.wait_ge(exps_done, 1)
            nc.tensor.transpose(ps[0][0:NT, 128:256], r0[:], g.ident[:]).then_inc(pe_rT, 1)
            for t in range(NT):
                last = nc.tensor.matmul(ps[6][0:F, 0:P], g.x_sb[:, t, :], g.ones[:], start=(t == 0),
                                        stop=(t == NT - 1))
            last.then_inc(pe_xsum, 1)
            pe.wait_ge(xsum_copied, 1)
            nc.tensor.matmul(ps[7][:, 0:F], xsum[:], g.w0_twice[0:F, :], start=True, stop=True).then_inc(pe_hsum, 1)
            pe.wait_ge(w_loaded, 16 * len(weights))
            for s in range(2):
                for d in range(DC):
                    nc.tensor.matmul(ps[2][0:F + 1, s * TYPES * H:(s + 1) * TYPES * H], qk[:, s, d, :],
                                     a_sb[:, s * DC + d, :], start=(d == 0), stop=(d == DC - 1))
            pe.wait_ge(fold_in, H + 1)
            for h in range(H):
                rows = slice((h % 2) * F, (h % 2 + 1) * F)
                nc.tensor.matmul(ps[3][rows, (h // 2) * F:(h // 2 + 1) * F], vwT_d[:, h, :], pw_sb[:, h, :],
                                 start=True, stop=True)
            nc.tensor.matmul(ps[4][:, 0:F], g.ones[0:1, :], pb_sb[:], start=True, stop=False)
            for h in range(H):
                last = nc.tensor.matmul(ps[4][:, 0:F], vb_bc[:, h, :], pw_sb[:, h, :], start=False,
                                        stop=(h == H - 1))
            last.then_inc(pe_fold, 1)


def layer0(nc, g):
    sem = g.sem
    code_ready = sem("code_ready")
    squared = sem("squared")
    transposed = sem("transposed")
    dense_ready = sem("dense_ready")
    t_ready = sem("t0_ready")
    multiplied = sem("multiplied")
    codes_out = sem("codes_out")
    codes_stored = [sem(f"codes_stored{n}") for n in range(2)]
    u_copied = sem("u_copied")
    num_ready, num_copied = sem("num_ready"), sem("num_copied")
    CREDIT = 4
    T_CREDIT = 2 * HALF_J
    with ExitStack() as local:
        code = g.sb("code", [P, 2, IT0, UNIT], BF16, local)
        junk = g.sb("junk", [P, IT0 * UNIT], BF16, local)
        dense = g.sb("dense", [P, HALF_J, IB0], F32, local)
        t0 = g.sb("t0", [P, 2, HALF_J, IB0], F32, local)
        code_t = g.sb("code_t", [P, 2, HALF_J, IB0], I8, local)
        u_sb = g.sb("u_sb", [P, 2, IB0], F32, local)
        tp = local.enter_context(nc.psum_tensor("tp", [P, 2, HALF_J, IB0], BF16))
        u_ps = local.enter_context(nc.psum_tensor("u_ps", [P, 2, IB0], F32))
        block = local.enter_context(nc.Block())
        NTB = IT0 // 2
        n_ps = [u_ps[:, 1, n * BANK:n * BANK + NTB * (F + 1)] for n in range(2)]

        @block.sync
        def _(sp):
            def load_block(b, first):
                for u in range(first, UNITS):
                    sp.wait_ge(code_ready, b * UNITS + (u + 1 - RAW))
                    load_adj(sp, g, b, u)

            load_block(0, RAW)
            with sp.Fori(1, NB0) as b:
                load_block(b, 0)

        @block.vector
        def _(dve):
            dve.sem_inc(t_ready, T_CREDIT)

            def clip(b, u):
                unit = b * UNITS + u
                dve.wait_ge(g.raw_loaded[u % RAW], b * (16 * UNITS // RAW) + 16 * (u // RAW + 1))
                dve.wait_ge(squared, unit + 1)
                dve.wait_ge(transposed, 2 * unit + 2)
                nc.vector.tensor_scalar(code[:, u % 2, :, :].rearrange("p t j -> p (t j)"),
                                        g.raw[:, u % RAW, :, :].rearrange("p t j -> p (t j)"),
                                        float(TYPES - 1), -1.0, ALU.min, ALU.max).then_inc(code_ready, 1)

            def block_of_targets(b, last_block):
                for u in range(UNITS):
                    for n in range(2):
                        half = (b * UNITS + u) * 2 + n
                        for a in range(HALF_J):
                            jt = (u * 2 + n) * HALF_J + a
                            dve.wait_ge(t_ready, half * HALF_J + (T_CREDIT - HALF_J + a + 1))
                            nc.vector.tensor_scalar(dense[:, a, :], g.r0_bc[:, bass.ds(b * IB0, IB0)],
                                                    g.tau0[:, jt:jt + 1], None, ALU.max).then_inc(dense_ready, 1)
                        dve.wait_ge(codes_out, half + 1)
                        dve.wait_ge(multiplied, half + 1)
                        for a in range(HALF_J):
                            dve.wait_ge(dense_ready, half * HALF_J + a + 1)
                            nc.vector.scalar_tensor_tensor(t0[:, n, a, :], code_t[:, n, a, :], 0.0, dense[:, a, :],
                                                           ALU.is_gt, ALU.mult).then_inc(t_ready, 1)
                        if n == 0 and u + 1 < UNITS:
                            clip(b, u + 1)
                        elif n == 0 and not last_block:
                            clip(b + 1, 0)

            clip(0, 0)
            with dve.Fori(0, NB0 - 1) as b:
                block_of_targets(b, False)
            block_of_targets(NB0 - 1, True)

        @block.scalar
        def _(act):
            act.sem_inc(squared, 2)
            for n in range(2):
                act.sem_inc(codes_stored[n], 16)
            with act.Fori(0, NB0) as b:
                for u in range(UNITS):
                    unit = b * UNITS + u
                    for n in range(2):
                        half = unit * 2 + n
                        act.wait_ge(transposed, half + 1 + CREDIT)
                        act.wait_ge(codes_stored[n], 16 * unit + 16)
                        act.wait_ge(t_ready, half * HALF_J + HALF_J)
                        nc.scalar.activation(code_t[:, n, :, :].rearrange("p a i -> p (a i)"),
                                             tp[:, n, :, :].rearrange("p a i -> p (a i)"),
                                             ACT.Copy).then_inc(codes_out, 1)
                        if n == 1:
                            nc.scalar.activation(junk[:], code[:, u % 2, :, :].rearrange("p t j -> p (t j)"),
                                                 ACT.Square, bias=g.minus_half[:],
                                                 accum_out=g.off_sum[:, bass.ds(unit, 1)]).then_inc(squared, 1)
                        act.wait_ge(codes_out, half + 1)
                        rows = (u * 2 + n) * HALF_J * P
                        dst = g.codes_dram[rows:rows + HALF_J * P, bass.ds(b * IB0, IB0)]
                        act.dma_start(dst.rearrange("(a p) i -> p a i", p=P),
                                      code_t[:, n, :, :]).then_inc(codes_stored[n], 16)
                act.wait_ge(multiplied, b * HALVES + HALVES + 2)
                for s in range(2):
                    nc.scalar.activation(u_sb[:, s, :], u_ps[:, s, :], ACT.Copy).then_inc(u_copied, 1)
                act.wait_ge(num_ready, b + 1)
                for n in range(2):
                    nc.scalar.activation(
                        g.num0[:].rearrange("p t c -> p (t c)")[
                            :, bass.ds(b * (IT0 * (F + 1)) + n * NTB * (F + 1), NTB * (F + 1))],
                        n_ps[n], ACT.Copy).then_inc(num_copied, 1)
            for n in range(2):
                act.wait_ge(codes_stored[n], 16 * (NB0 * UNITS + 1))

        @block.tensor
        def _(pe):
            pe.sem_inc(transposed, CREDIT)
            pe.sem_inc(multiplied, 2)

            def transpose(b, u, n):
                half = (b * UNITS + u) * 2 + n
                if n == 0:
                    pe.wait_ge(code_ready, b * UNITS + u + 1)
                if not isinstance(half, int) or half >= 2:
                    pe.wait_ge(codes_out, half - 1)
                for a in range(HALF_J):
                    for t in range(IT0):
                        j = (n * HALF_J + a) * P
                        last = nc.tensor.transpose(tp[:, n, a, t * P:(t + 1) * P], code[:, u % 2, t, j:j + P],
                                                   g.ident_b[:])
                last.then_inc(transposed, 1)

            def multiply(b, u, n):
                half = (b * UNITS + u) * 2 + n
                if u == 0 and n == 0 and (not isinstance(b, int) or b >= 1):
                    pe.wait_ge(num_copied, 2 * b)
                pe.wait_ge(t_ready, half * HALF_J + (T_CREDIT + HALF_J))
                jt = (u * 2 + n) * HALF_J
                for c in range(0, IB0, BANK):
                    for a in range(HALF_J):
                        nc.tensor.matmul(u_ps[a * F:(a + 1) * F, 0, c:c + BANK], g.x0_w[:, jt + a, :],
                                         t0[:, n, a, c:c + BANK], start=(jt == 0), stop=(jt == NT - HALF_J))
                for c in range(0, IB0, BANK):
                    for a in range(HALF_J):
                        r = (jt + a) % 4 * 32
                        last = nc.tensor.matmul(u_ps[r:r + 32, 1, c:c + BANK], g.w0_rep[:, jt + a, :],
                                                t0[:, n, a, c:c + BANK], start=(jt < 4), stop=(jt >= NT - 4))
                last.then_inc(multiplied, 1)

            order = [(u, n) for u in range(UNITS) for n in range(2)]

            def block_of_targets(b, last_block):
                for m, (u, n) in enumerate(order):
                    if m + 1 < HALVES:
                        transpose(b, *order[m + 1])
                    elif not last_block:
                        transpose(b + 1, 0, 0)
                    multiply(b, u, n)
                pe.wait_ge(u_copied, 2 * b + 2)
                for t in range(IT0):
                    n, c = t // NTB, t % NTB * (F + 1)
                    nc.tensor.matmul(n_ps[n][:, c:c + F], u_sb[:, 0, t * P:(t + 1) * P], g.w0_twice[:],
                                     start=True, stop=True)
                    last = nc.tensor.matmul(n_ps[n][:, c + F:c + F + 1], u_sb[:, 1, t * P:(t + 1) * P],
                                            g.den_rows[:], start=True, stop=True)
                last.then_inc(num_ready, 1)

            transpose(0, 0, 0)
            block_of_targets(0, False)
            with pe.Fori(1, NB0 - 1) as b:
                block_of_targets(b, False)
            block_of_targets(NB0 - 1, True)


def between(nc, g):
    sem = g.sem
    dve_step, tables_step = sem("between_dve_step"), sem("tables_dve_step")
    elu_in, elu_exp = sem("elu_in"), sem("elu_exp")
    centered, squares, var_ready, root = sem("centered0"), sem("squares0"), sem("var0"), sem("root0")
    ones_set, one_copied = sem("ones_set"), sem("x1_one_copied")
    x1_ready, xT_made, xT_copied = sem("x1_ready"), sem("x1T_made"), sem("x1T_copied")
    s_made, s_copied = sem("s_made"), sem("s_copied")
    max_ready, max_made, beta_diag, beta_made = sem("b_max"), sem("b_maxT"), sem("beta_diag"), sem("beta_made")
    expo_ready, exps_done = sem("expo1_ready"), sem("exps1_done")
    rows_made, rows_copied, rows_stored = sem("rows_made"), sem("rows_copied"), sem("rows_stored")
    flag_max, flag_T, flag_row = sem("flag_max"), sem("flag_T"), sem("flag_row")
    TG = BANK // P
    BANKS = 7
    with ExitStack() as local:
        z = g.sb("z", [P, NT], F32, local)
        den = g.sb("den", [P, NT], F32, local)
        rec = g.sb("rec", [P, NT], F32, local)
        ha = g.sb("ha", [P, NT, F], F32, local)
        hb = g.sb("hb", [P, NT, F], F32, local)
        x1T = g.sb("x1T", [F + 1, N], F32, local)
        s12_all = g.sb("s12", [P, NT * 2 * KH], F32, local)
        b_max = g.sb("b_max", [P, KH], F32, local)
        beta_col = g.sb("beta_col", [KH, 1], F32, local)
        beta_d = g.sb("beta_d", [KH, KH], F32, local)
        beta_r = g.sb("beta_r", [P, KH], F32, local)
        e_r_all = g.sb("e_r", [P, NT * KH], F32, local)
        e_t_all = g.sb("e_t", [P, NT * KH], F32, local)
        e_c_all = g.sb("e_c", [P, NT * KH], F32, local)
        m_max = g.sb("m_max", [P, NT, H], F32, local)
        rowsT = g.sb("rowsT", [KH, 2, N], F32, local)
        off_max = g.sb("off_max", [P, 1], F32, local)
        off_row = g.sb("off_row", [1, 1], F32, local)
        ps = [local.enter_context(nc.psum_tensor(f"mid_ps{i}", [P, BANK], F32)) for i in range(8)]
        block = local.enter_context(nc.Block())
        x1_one = g.x1_one[:].rearrange("p (t c) -> p t c", c=F)

        def tables(kinds):
            wide = kinds * H

            def table(ap):
                return ap[:, 0:NT * wide].rearrange("p (t c) -> p t c", c=wide)

            s12 = s12_all[:, 0:NT * 2 * wide].rearrange("p (t s c) -> p t s c", s=2, c=wide)
            return wide, s12, table(e_r_all), table(e_t_all), table(e_c_all)

        def score_groups(wide):
            tiles = min(BANK // (2 * wide), 8)
            return tiles, -(-NT // tiles)

        @block.gpsimd
        def _(pool):
            pool.memset(x1T[F:F + 1, :], 1.0).then_inc(ones_set, 1)
            pool.wait_ge(ones_set, 1)
            pool.memset(x1_one[:, :, F - 1:F], 1.0).then_inc(ones_set, 1)

        @block.vector
        def _(dve):
            step = Chain(dve, dve_step)
            nc.vector.tensor_reduce(off_max[:], g.off_sum[:], AX.X, ALU.max).then_inc(flag_max, 1)
            step(nc.vector.tensor_scalar(z[:], g.num0[:, :, F], 0.0, None, ALU.is_equal))
            step(nc.vector.scalar_tensor_tensor(den[:], z[:], float(N), g.num0[:, :, F], ALU.mult, ALU.add))
            step(nc.vector.reciprocal(rec[:], den[:]))
            step(nc.vector.tensor_tensor(ha[:], over_rows(g.hsum[:], [P, NT, F]), over_columns(z[:], [P, NT, F]),
                                         ALU.mult))
            step(nc.vector.tensor_tensor(ha[:], ha[:], g.num0[:, :, 0:F], ALU.add))
            step(nc.vector.tensor_tensor(ha[:], ha[:], over_columns(rec[:], [P, NT, F]), ALU.mult))
            nc.vector.tensor_scalar(hb[:], ha[:], 0.0, None, ALU.min).then_inc(elu_in, 1)
            dve.wait_ge(flag_T, 1)
            step(nc.vector.tensor_reduce(off_row[:], ps[7][0:1, 0:P], AX.X, ALU.max))
            quiet = float(IT0 * UNIT) / 4.0
            nc.vector.tensor_scalar(g.general[:], off_row[:], quiet, None, ALU.is_gt).then_inc(flag_row, 1)
            step(nc.vector.scalar_tensor_tensor(ha[:], ha[:], 0.0, g.x_sb[:], ALU.max, ALU.add))
            dve.wait_ge(elu_exp, 1)
            step(nc.vector.scalar_tensor_tensor(ha[:], hb[:], -1.0, ha[:], ALU.add, ALU.add))
            step(nc.vector.tensor_reduce(z[:], ha[:], AX.X, ALU.add))
            step(nc.vector.tensor_scalar(z[:], z[:], 1.0 / F, None, ALU.mult))
            nc.vector.tensor_tensor(ha[:], ha[:], over_columns(z[:], [P, NT, F]), ALU.subtract).then_inc(centered, 1)
            dve.wait_ge(squares, 1)
            step(nc.vector.tensor_reduce(den[:], hb[:], AX.X, ALU.add))
            nc.vector.tensor_scalar(den[:], den[:], 1.0 / F, EPS, ALU.mult, ALU.add).then_inc(var_ready, 1)
            dve.wait_ge(root, 1)
            step(nc.vector.reciprocal(rec[:], rec[:]))
            nc.vector.tensor_tensor(g.x1[:], ha[:], over_columns(rec[:], [P, NT, F]), ALU.mult).then_inc(x1_ready, 1)
            for n in range(NT // TG):
                dve.wait_ge(xT_made, n + 1)
                nc.vector.tensor_copy(x1T[0:F, n * TG * P:(n + 1) * TG * P],
                                      ps[n % BANKS][0:F, :]).then_inc(xT_copied, 1)
            dve.wait_ge(flag_row, 1)

            def program(kinds):
                step = Chain(dve, tables_step)
                wide, s12, e_r, e_t, e_c = tables(kinds)
                tiles, groups = score_groups(wide)
                for n in range(groups):
                    m = min(tiles, NT - n * tiles)
                    dve.wait_ge(s_made, n + 1)
                    nc.vector.tensor_copy(s12[:, n * tiles:n * tiles + m, :, :].rearrange("p t s c -> p (t s c)"),
                                          ps[n % BANKS][:, 0:m * 2 * wide]).then_inc(s_copied, 1)
                dve.wait_ge(s_copied, groups)
                nc.vector.tensor_reduce(b_max[:, 0:wide], s12[:, :, 1, :].rearrange("p t c -> p c t"), AX.X,
                                        ALU.max).then_inc(max_ready, 1)
                dve.wait_ge(max_made, 1)
                step(nc.vector.tensor_reduce(beta_col[0:wide, :], ps[7][0:wide, 0:P], AX.X, ALU.max))
                nc.vector.tensor_scalar(beta_d[0:wide, 0:wide], g.ident[0:wide, 0:wide], beta_col[0:wide, :], None,
                                        ALU.mult).then_inc(beta_diag, 1)
                dve.wait_ge(beta_made, 1)
                step(nc.vector.tensor_copy(beta_r[:, 0:wide], ps[7][:, P:P + wide]))
                shape = [P, NT, wide]
                step(nc.vector.tensor_tensor(e_r, s12[:, :, 0, :], over_rows(beta_r[:, 0:wide], shape), ALU.add))
                step(nc.vector.scalar_tensor_tensor(e_c, e_r, SLOPE1, e_r, ALU.mult, ALU.max))
                step(nc.vector.tensor_scalar(e_r, e_r, 1.0 - SLOPE1, LIMIT, ALU.mult, ALU.min))
                step(nc.vector.tensor_tensor(e_t, s12[:, :, 1, :], over_rows(beta_r[:, 0:wide], shape),
                                             ALU.subtract))
                nc.vector.tensor_scalar(e_t, e_t, -LIMIT, None, ALU.max).then_inc(expo_ready, 1)
                step(nc.vector.tensor_reduce(m_max[:], e_c.rearrange("p t (k h) -> p t h k", h=H), AX.X, ALU.max))
                for k in range(kinds):
                    cols = slice(k * H, (k + 1) * H)
                    step(nc.vector.tensor_tensor(e_c[:, :, cols], e_c[:, :, cols], m_max[:], ALU.subtract))
                step(nc.vector.tensor_scalar(s12[:, :, 0, :], e_r, 0.0, None, ALU.max))
                nc.vector.tensor_tensor(e_c, e_c, s12[:, :, 0, :], ALU.subtract).then_inc(expo_ready, 1)
                for n in range(2 * NT // TG):
                    s, m = divmod(n, NT // TG)
                    dve.wait_ge(rows_made, n + 1)
                    nc.vector.tensor_copy(rowsT[0:wide, s, m * TG * P:(m + 1) * TG * P],
                                          ps[n % BANKS][0:wide, :]).then_inc(rows_copied, 1)

            either(dve, g, program)

        @block.scalar
        def _(act):
            act.wait_ge(elu_in, 1)
            nc.scalar.activation(hb[:], hb[:], ACT.Exp).then_inc(elu_exp, 1)
            act.wait_ge(centered, 1)
            nc.scalar.activation(hb[:], ha[:], ACT.Square).then_inc(squares, 1)
            act.wait_ge(var_ready, 1)
            nc.scalar.activation(rec[:], den[:], ACT.Sqrt).then_inc(root, 1)
            act.wait_ge(x1_ready, 1)
            nc.scalar.activation(x1_one[:, :, 0:F - 1], g.x1[:, :, 0:F - 1], ACT.Copy).then_inc(one_copied, 1)
            act.wait_ge(flag_row, 1)

            def program(kinds):
                wide, s12, e_r, e_t, e_c = tables(kinds)
                act.wait_ge(expo_ready, 1)
                nc.scalar.activation(g.tau[:, 0:NT * wide], e_t_all[:, 0:NT * wide], ACT.Exp,
                                     scale=-(1.0 - SLOPE1)).then_inc(exps_done, 1)
                nc.scalar.activation(g.w_exp[:, 0:NT * wide], e_t_all[:, 0:NT * wide], ACT.Exp).then_inc(exps_done, 1)
                act.wait_ge(expo_ready, 2)
                nc.scalar.activation(e_r, e_r, ACT.Exp).then_inc(exps_done, 1)
                nc.scalar.activation(e_c, e_c, ACT.Exp).then_inc(exps_done, 1)

            either(act, g, program)

        @block.tensor
        def _(pe):
            pe.wait_ge(flag_max, 1)
            nc.tensor.transpose(ps[7][0:1, 0:P], off_max[:], g.ident[:]).then_inc(flag_T, 1)
            pe.wait_ge(x1_ready, 1)
            for n in range(NT // TG):
                if n >= BANKS:
                    pe.wait_ge(xT_copied, n - BANKS + 1)
                for t in range(TG):
                    last = nc.tensor.transpose(ps[n % BANKS][0:F, t * P:(t + 1) * P], g.x1[:, n * TG + t, :],
                                               g.ident[:])
                last.then_inc(xT_made, 1)
            pe.wait_ge(ones_set, 2)
            pe.wait_ge(flag_row, 1)

            def program(kinds):
                wide, s12, e_r, e_t, e_c = tables(kinds)
                tiles, groups = score_groups(wide)
                folded = g.g_fold[:].rearrange("c (s k) -> c s k", s=2)[:, :, 0:wide]
                pe.wait_ge(xT_copied, NT // TG)
                for n in range(groups):
                    m = min(tiles, NT - n * tiles)
                    if n >= BANKS:
                        pe.wait_ge(s_copied, n - BANKS + 1)
                    for t in range(m):
                        it = n * tiles + t
                        last = nc.tensor.matmul(ps[n % BANKS][:, t * 2 * wide:(t + 1) * 2 * wide],
                                                x1T[:, it * P:(it + 1) * P], folded, start=True, stop=True)
                    last.then_inc(s_made, 1)
                pe.wait_ge(max_ready, 1)
                nc.tensor.transpose(ps[7][0:wide, 0:P], b_max[:, 0:wide], g.ident[:]).then_inc(max_made, 1)
                pe.wait_ge(beta_diag, 1)
                nc.tensor.matmul(ps[7][:, P:P + wide], g.ones[0:wide, :], beta_d[0:wide, 0:wide], start=True,
                                 stop=True).then_inc(beta_made, 1)
                for n in range(2 * NT // TG):
                    s, m = divmod(n, NT // TG)
                    if m == 0:
                        pe.wait_ge(exps_done, 3 + s)
                    if n >= BANKS:
                        pe.wait_ge(rows_copied, n - BANKS + 1)
                    for t in range(TG):
                        last = nc.tensor.transpose(ps[n % BANKS][0:wide, t * P:(t + 1) * P],
                                                   (e_r, e_c)[s][:, m * TG + t, :], g.ident[:])
                    last.then_inc(rows_made, 1)

            either(pe, g, program)

        @block.sync
        def _(sp):
            sp.wait_ge(flag_row, 1)

            def program(kinds):
                for s, dst in enumerate((g.r_dram, g.c_dram)):
                    sp.wait_ge(rows_copied, (s + 1) * (NT // TG))
                    sp.dma_start(dst[0:kinds * H, :], rowsT[0:kinds * H, s, :]).then_inc(rows_stored, 16)
                sp.wait_ge(rows_stored, 32)

            either(sp, g, program)


def layer1(nc, g):
    sem = g.sem
    codes_loaded = [sem(f"codes_loaded{n}") for n in range(UNROLL)]
    rows_loaded = [sem(f"rows_loaded{h}") for h in range(HG)]
    factors_loaded = sem("factors_loaded")
    kind_set = sem("kind_set")
    mask_square = sem("mask_square")
    mask_ready = sem("mask_ready")
    w_ready = sem("w_ready")
    t_ready = sem("t1_ready")
    pairs_done = sem("pairs_done")
    weighed = sem("weighed")
    sums_stored = sem("sums_stored")
    T_CREDIT = UNROLL * HG
    P_CREDIT = UNROLL * PAIRS
    FACTORS_AT = 4
    with ExitStack() as local:
        rows = g.sb("rows", [P, HG, IB1], F32, local)
        factors = g.sb("factors", [P, PAIRS, IB1], F32, local)
        u_sb = g.sb("u1_sb", [P, PAIRS, IB1], F32, local)
        t1 = g.sb("t1", [P, PAIRS, 2, IB1], F32, local)
        mask = g.sb("mask", [P, UNROLL, IB1], BF16, local)
        kind = g.sb("kind", [P, 1], F32, local)
        off_kind = g.sb("off_kind", [P, 2, IB1], BF16, local)
        codes = g.sb("codes", [P, UNROLL, IB1], I8, local)
        x_w = g.sb("x_w", [P, UNROLL, HG, F], F32, local)
        u_ps = local.enter_context(nc.psum_tensor("u1_ps", [P, PAIRS, IB1], F32))
        block = local.enter_context(nc.Block())

        def passes(eng, kinds, one_pass, peel_first=False):
            def visit(v, first):
                one_pass(v, 0, v * kinds, *first)
                if kinds > 2:
                    with eng.Fori(1, kinds - 1) as k:
                        one_pass(v, k, v * kinds + k)
                one_pass(v, kinds - 1, v * kinds + (kinds - 1))

            if peel_first:
                visit(0, (True,))
                with eng.Fori(1, VISITS) as v:
                    visit(v, ())
            else:
                with eng.Fori(0, VISITS) as v:
                    visit(v, ())

        @block.sync
        def _(sp):
            sp.sem_inc(sums_stored, 16)

            def program(kinds):
                def load_codes(v, s, number):
                    b = v // GROUPS
                    for n in range(UNROLL):
                        sp.wait_ge(mask_ready, number * UNROLL + n + 1)
                        src = g.codes_dram[bass.ds((s * UNROLL + n) * P, P), bass.ds(b * IB1, IB1)]
                        sp.dma_start(codes[:, n, :], src).then_inc(codes_loaded[n], 16)

                def store_sums(p):
                    sp.wait_ge(weighed, p * PAIRS + PAIRS)
                    dst = g.acc_dram[bass.ds(p, 1), :, :, :].rearrange("v p q i -> (v p) (q i)")
                    sp.dma_start(dst, u_sb[:].rearrange("p q i -> p (q i)")).then_inc(sums_stored, 16)

                def one_pass(v, k, p, first=False):
                    b, group = v // GROUPS, v % GROUPS
                    for h in range(HG):
                        sp.wait_ge(t_ready, p * (NT * HG) + (T_CREDIT - HG + h + 1))
                        src = g.r_dram[bass.ds(k * H + group * HG + h, 1), bass.ds(b * IB1, IB1)]
                        sp.dma_start(rows[:, h, :], src.to_broadcast([P, IB1])).then_inc(rows_loaded[h], 16)
                    with sp.Fori(1, FACTORS_AT) as s:
                        load_codes(v, s, p * STEPS + s)
                    if not first:
                        store_sums(p - 1)
                    for q in range(PAIRS):
                        for s in range(2):
                            src = g.c_dram[bass.ds(k * H + group * HG + (2 * q + s), 1), bass.ds(b * IB1, IB1)]
                            sp.dma_start(factors[s * F:(s + 1) * F, q, :],
                                         src.to_broadcast([F, IB1])).then_inc(factors_loaded, 16)
                    last_kind = isinstance(k, int) and k == kinds - 1
                    with sp.Fori(FACTORS_AT, STEPS + 1) as s:
                        load_codes((v + s // STEPS) % VISITS if last_kind else v, s % STEPS, p * STEPS + s)

                load_codes(0, 0, 0)
                passes(sp, kinds, one_pass, peel_first=True)
                store_sums(VISITS * kinds - 1)
                sp.wait_ge(sums_stored, 16 * (VISITS * kinds + 1))
                for n in range(UNROLL):
                    sp.wait_ge(codes_loaded[n], 16 * (VISITS * kinds * STEPS + 1))

            either(sp, g, program)

        @block.scalar
        def _(act):
            act.sem_inc(mask_ready, UNROLL)

            def program(kinds):
                wide = kinds * H

                def set_kind(k, number):
                    nc.scalar.activation(kind[:], g.neg_kind[:, bass.ds(k, 1)], ACT.Copy).then_inc(kind_set, 1)
                    act.wait_ge(kind_set, number + 1)

                def make_masks(v, k, s, number):
                    for n in range(UNROLL):
                        tile = number * UNROLL + n
                        act.wait_ge(pairs_done, tile * PAIRS + PAIRS)
                        act.wait_ge(t_ready, tile * HG + HG)
                        act.wait_ge(mask_ready, tile + (UNROLL - 1))
                        act.wait_ge(codes_loaded[n], 16 * number + 16)
                        nc.scalar.activation(off_kind[:, n % 2, :], codes[:, n, :], ACT.Square,
                                             bias=kind[:]).then_inc(mask_square, 1)
                        for h in range(HG):
                            col = (s * UNROLL + n) * wide + k * H + (v % GROUPS) * HG + h
                            last = nc.scalar.activation(x_w[:, n, h, :], g.x1_one[:, bass.ds((s * UNROLL + n) * F, F)],
                                                        ACT.Copy, scale=g.w_exp[:, bass.ds(col, 1)])
                        last.then_inc(w_ready, 1)
                        act.wait_ge(mask_square, tile + 1)
                        nc.scalar.activation(mask[:, n, :], off_kind[:, n % 2, :], ACT.Relu, bias=1.0,
                                             scale=-1.0).then_inc(mask_ready, 1)

                def one_pass(v, k, p):
                    with act.Fori(1, STEPS) as s:
                        make_masks(v, k, s, p * STEPS + s)
                    last_kind = isinstance(k, int) and k == kinds - 1
                    k_next = 0 if last_kind else k + 1
                    set_kind(k_next, p + 1)
                    make_masks(v + 1 if last_kind else v, k_next, 0, (p + 1) * STEPS)

                set_kind(0, 0)
                make_masks(0, 0, 0, 0)
                passes(act, kinds, one_pass)

            either(act, g, program)

        @block.vector
        def _(dve):
            dve.sem_inc(t_ready, T_CREDIT)

            def program(kinds):
                wide = kinds * H

                def one_pass(v, k, p):
                    def step(s, first):
                        for n in range(UNROLL):
                            tile = p * NT + s * UNROLL + n
                            dve.wait_ge(mask_ready, tile + 1 + UNROLL)
                            for h in range(HG):
                                q = h // 2
                                if h % 2 == 0:
                                    dve.wait_ge(pairs_done, tile * PAIRS + (P_CREDIT - PAIRS + q + 1))
                                if first and n == 0:
                                    dve.wait_ge(rows_loaded[h], 16 * p + 16)
                                col = (s * UNROLL + n) * wide + k * H + (v % GROUPS) * HG + h
                                nc.vector.scalar_tensor_tensor(
                                    t1[:, q, h % 2, :], rows[:, h, :], g.tau[:, bass.ds(col, 1)], mask[:, n, :],
                                    ALU.max, ALU.mult).then_inc(t_ready, 1)

                    step(0, True)
                    with dve.Fori(1, STEPS) as s:
                        step(s, False)
                    dve.wait_ge(factors_loaded, (p + 1) * (16 * HG))
                    dve.wait_ge(sums_stored, p * 16 + 16)
                    for q in range(PAIRS):
                        dve.wait_ge(pairs_done, p * (NT * PAIRS) + (P_CREDIT + (NT - 1) * PAIRS + q + 1))
                        nc.vector.tensor_tensor(u_sb[:, q, :], u_ps[:, q, :], factors[:, q, :],
                                                ALU.mult).then_inc(weighed, 1)

                passes(dve, kinds, one_pass)

            either(dve, g, program)

        @block.tensor
        def _(pe):
            pe.sem_inc(pairs_done, P_CREDIT)

            def program(kinds):
                def multiply(tile, p, n, first, last_tile):
                    pe.wait_ge(w_ready, tile + 1)
                    for q in range(PAIRS):
                        pe.wait_ge(t_ready, tile * HG + (T_CREDIT + 2 * q + 2))
                        if first and (not isinstance(p, int) or p >= 1):
                            pe.wait_ge(weighed, p * PAIRS - PAIRS + q + 1)
                        for c in range(0, IB1, BANK):
                            for s in range(2):
                                last = nc.tensor.matmul(u_ps[s * F:(s + 1) * F, q, c:c + BANK],
                                                        x_w[:, n, 2 * q + s, :], t1[:, q, s, c:c + BANK],
                                                        start=first, stop=last_tile)
                        last.then_inc(pairs_done, 1)

                def one_pass(v, k, p, first=False):
                    for n in range(UNROLL):
                        multiply(p * NT + n, p, n, n == 0, False)
                    with pe.Fori(1, STEPS - 1) as s:
                        for n in range(UNROLL):
                            multiply(p * NT + s * UNROLL + n, p, n, False, False)
                    for n in range(UNROLL):
                        multiply(p * NT + ((STEPS - 1) * UNROLL + n), p, n, False, n == UNROLL - 1)

                passes(pe, kinds, one_pass, peel_first=True)

            either(pe, g, program)


def final(nc, g):
    sem = g.sem
    sums_loaded = [sem(f"sums_loaded{n}") for n in range(2)]
    projected, divided = sem("projected"), sem("divided")
    y_read = sem("y_read")
    rden_step, dve_step = sem("final_rden_step"), sem("final_dve_step")
    centered, squares, var_ready, root = sem("centered1"), sem("squares1"), sem("var1"), sem("root1")
    out_ready, out_stored = sem("out_ready"), sem("out_stored")
    ITC = 2
    CHUNKS = NT // ITC
    SLOTS = 2
    HP = H // 2
    WIDE = 256
    with ExitStack() as local:
        sums = g.sb("sums_in", [P, SLOTS, KINDS, HP, ITC * P], F32, local)
        rden = g.sb("rden", [P, SLOTS, ITC * HP, 2], F32, local)
        y = g.sb("y", [P, SLOTS, ITC, H, F], F32, local)
        o = g.sb("o", [P, NT, F], F32, local)
        sq = g.sb("sq", [P, NT, F], F32, local)
        mean = g.sb("mean", [P, NT], F32, local)
        var = g.sb("var", [P, NT], F32, local)
        rec = g.sb("rec1", [P, NT], F32, local)
        ps = local.enter_context(nc.psum_tensor("fin_ps", [P, SLOTS, ITC * HP, WIDE], F32))
        block = local.enter_context(nc.Block())

        @block.sync
        def _(sp):
            def program(kinds):
                for c in range(CHUNKS):
                    b, i = divmod(c * ITC * P, IB1)
                    if c >= SLOTS:
                        sp.wait_ge(projected, c - SLOTS + 1)
                    for group in range(GROUPS):
                        p = (b * GROUPS + group) * kinds
                        for q in range(PAIRS):
                            src = g.acc_dram[p:p + kinds, :, q, i:i + ITC * P].rearrange("k p i -> p k i")
                            sp.dma_start(sums[:, c % SLOTS, 0:kinds, group * PAIRS + q, :],
                                         src).then_inc(sums_loaded[c % SLOTS], 16)

            either(sp, g, program)
            sp.wait_ge(out_ready, 1)
            sp.dma_start(g.out.rearrange("(t p) c -> p t c", p=P), o[:]).then_inc(out_stored, 16)
            sp.wait_ge(out_stored, 16)

        @block.tensor
        def _(pe):
            def program(kinds):
                for c in range(CHUNKS):
                    n = c % SLOTS
                    pe.wait_ge(sums_loaded[n], 16 * HP * (c // SLOTS + 1))
                    if c >= SLOTS:
                        pe.wait_ge(divided, c - SLOTS + 1)
                    for t in range(ITC):
                        for q in range(HP):
                            for k in range(kinds):
                                last = nc.tensor.matmul(ps[:, n, t * HP + q, 0:2 * F + 2],
                                                        sums[:, n, k, q, t * P:(t + 1) * P], g.vp_fold[:, q, :],
                                                        start=(k == 0), stop=(k == kinds - 1))
                    last.then_inc(projected, 1)

            either(pe, g, program)

        @block.vector
        def _(dve):
            def add_heads(c):
                dve.wait_ge(divided, c + 1)
                nc.vector.tensor_reduce(o[:, c * ITC:(c + 1) * ITC, :],
                                        y[:, c % SLOTS, :, :, :].rearrange("p t h c -> p t c h"), AX.X,
                                        ALU.add).then_inc(y_read, 1)

            for c in range(CHUNKS):
                n = c % SLOTS
                dve.wait_ge(projected, c + 1)
                nc.vector.reciprocal(rden[:, n, :, :], ps[:, n, :, 2 * F:2 * F + 2]).then_inc(rden_step, 1)
                if c >= 1:
                    add_heads(c - 1)
                heads = ps[:, n, :, 0:2 * F].rearrange("p m (s c) -> p m s c", s=2)
                shape = [P, ITC * HP, 2, F]
                dve.wait_ge(rden_step, c + 1)
                if c >= SLOTS:
                    dve.wait_ge(y_read, c - SLOTS + 1)
                nc.vector.tensor_tensor(y[:, n, :, :, :].rearrange("p t (q s) c -> p (t q) s c", s=2), heads,
                                        rden[:, n, :, :].unsqueeze(3).to_broadcast(shape),
                                        ALU.mult).then_inc(divided, 1)
            add_heads(CHUNKS - 1)
            dve.wait_ge(y_read, CHUNKS)
            step = Chain(dve, dve_step)
            step(nc.vector.tensor_tensor(o[:], o[:], g.x1[:], ALU.add))
            step(nc.vector.tensor_tensor(o[:], o[:], over_rows(g.out_bias[:], [P, NT, F]), ALU.add))
            step(nc.vector.tensor_reduce(mean[:], o[:], AX.X, ALU.add))
            step(nc.vector.tensor_scalar(mean[:], mean[:], 1.0 / F, None, ALU.mult))
            nc.vector.tensor_tensor(o[:], o[:], over_columns(mean[:], [P, NT, F]), ALU.subtract).then_inc(centered, 1)
            dve.wait_ge(squares, 1)
            step(nc.vector.tensor_reduce(var[:], sq[:], AX.X, ALU.add))
            nc.vector.tensor_scalar(var[:], var[:], 1.0 / F, EPS, ALU.mult, ALU.add).then_inc(var_ready, 1)
            dve.wait_ge(root, 1)
            step(nc.vector.reciprocal(rec[:], rec[:]))
            nc.vector.tensor_tensor(o[:], o[:], over_columns(rec[:], [P, NT, F]), ALU.mult).then_inc(out_ready, 1)

        @block.scalar
        def _(act):
            act.wait_ge(centered, 1)
            nc.scalar.activation(sq[:], o[:], ACT.Square).then_inc(squares, 1)
            act.wait_ge(var_ready, 1)
            nc.scalar.activation(rec[:], var[:], ACT.Sqrt).then_inc(root, 1)


def kernel(**inputs):
    import numpy as np
    import concourse.bacc as bacc
    from concourse.bass_utils import run_bass_kernel_spmd

    def laid(a):
        return np.ascontiguousarray(a)

    given = {name: np.asarray(a) for name, a in inputs.items()}
    x, adj, w0 = given["x"], given["adj"], given["L0_gnn_W"]
    arrays = {
        "x": laid(x), "xT": laid(x.T), "adj": laid(adj), "w0": laid(w0), "w0T": laid(w0.T),
        "a12": laid(given["L0_gnn_a"].reshape(2, F).T),
        "qwT": laid(given["L1_gnn_Qw"].T), "qb": laid(given["L1_gnn_Qb"]),
        "kwT": laid(given["L1_gnn_Kw"].T), "kb": laid(given["L1_gnn_Kb"]),
        "vwT": laid(given["L1_gnn_Vw"].T), "vb": laid(given["L1_gnn_Vb"]),
        "a_cat": laid(given["L1_gnn_a"].transpose(1, 0, 2).reshape(2 * D1, TYPES * H)),
        "pw": laid(given["L1_gnn_Pw"]), "pb": laid(given["L1_gnn_Pb"]),
    }
    nc = bacc.Bacc("TRN2", target_bir_lowering=False, num_devices=1)
    args = {name: nc.dram_tensor(f"in_{name}", a.shape, mybir.dt.from_np(a.dtype), kind="ExternalInput").ap()
            for name, a in arrays.items()}
    out = nc.dram_tensor("out_nodes", (N, F), F32, kind="ExternalOutput").ap()
    gat_program(nc, out=out, **args)
    result = run_bass_kernel_spmd(nc, [{f"in_{name}": a for name, a in arrays.items()}], core_ids=[0])
    return result.results[0]["out_nodes"]
```

```python
from contextlib import ExitStack

import concourse.bass as bass
from concourse import mybir

F32 = mybir.dt.float32
BF16 = mybir.dt.bfloat16
I8 = mybir.dt.int8
I32 = mybir.dt.int32
ALU = mybir.AluOpType
ACT = mybir.ActivationFunctionType
AX = mybir.AxisListType

P = 128
N = 4096
F = 64
NT = N // P
H = 8
TYPES = 8
KINDS = TYPES + 1
KH = KINDS * H
D1 = F * H
DC = D1 // P
SLOPE0 = 0.01
SLOPE1 = 0.2
EPS = 1e-5
LIMIT = 80.0

IB0 = 1024
IT0 = IB0 // P
UNIT = 512
UNITS = N // UNIT
HALF_J = 2
HALVES = 2 * UNITS
NB0 = N // IB0
RAW = 4
CAPPED = (1, 0)
CAP = 2.0 ** 120
BANK = 512

IB1 = 2048
NB1 = N // IB1
HG = 4
GROUPS = H // HG
VISITS = NB1 * GROUPS
PAIRS = HG // 2
UNROLL = 4
STEPS = NT // UNROLL


class Shared:
    pass


def gat_program(nc, x, xT, adj, w0, w0T, a12, qwT, qb, kwT, kb, vwT, vb, a_cat, pw, pb, out):
    ctx = ExitStack()
    g = Shared()
    g.x, g.xT, g.adj, g.w0, g.w0T, g.a12, g.out = x, xT, adj, w0, w0T, a12, out
    g.qwT, g.qb, g.kwT, g.kb, g.vwT, g.vb, g.a_cat, g.pw, g.pb = qwT, qb, kwT, kb, vwT, vb, a_cat, pw, pb

    def dram(name, shape, dt):
        return nc.dram_tensor(name, shape, dt).ap()

    g.codes_dram = dram("codes_t", (N, N), I8)
    g.r_dram = dram("r_rows", (KH, N), F32)
    g.c_dram = dram("c_rows", (KH, N), F32)
    g.acc_dram = dram("acc_t", (VISITS, P, PAIRS, IB1), F32)

    with ctx:
        def sb(name, shape, dt, stack=ctx):
            return stack.enter_context(nc.sbuf_tensor(name, shape, dt))

        def sem(name):
            return ctx.enter_context(nc.semaphore(name))

        g.sb, g.sem = sb, sem
        g.ident = sb("ident", [P, P], F32)
        g.ident_b = sb("ident_b", [P, P], BF16)
        g.ones = sb("ones", [P, P], F32)
        g.neg_kind = sb("neg_kind", [P, KINDS], F32)
        g.minus_half = sb("minus_half", [P, 1], F32)
        g.g_fold = sb("g_fold", [P, 2 * KH], F32)
        g.vp_fold = sb("vp_fold", [P, H // 2, 2 * F + 2], F32)
        g.out_bias = sb("out_bias", [P, F], F32)
        g.general = sb("general", [1, 1], I32)
        g.x_sb = sb("x_sb", [P, NT, F], F32)
        g.u_all = sb("u0_all", [P, 2, N], F32)
        g.w0_twice = sb("w0_twice", [P, F], F32)
        g.den_rows = sb("den_rows", [P, 1], F32)
        g.hsum = sb("hsum", [P, F], F32)
        g.off_sum = sb("off_sum", [P, NB0 * HALVES], F32)
        with ExitStack() as first:
            g.tau0 = sb("tau0", [P, NT], F32, first)
            g.x0_w = sb("x0_w", [P, NT, F], F32, first)
            g.w0_rep = sb("w0_rep", [P, NT, 32], F32, first)
            g.r0_bc = sb("r0_bc", [P, N], F32, first)
            g.raw = sb("raw", [P, RAW, IT0, UNIT], I32, first)
            g.raw_loaded = [sem(f"raw_loaded{n}") for n in range(RAW)]
            prepare(nc, g)
            layer0(nc, g)
        g.x1 = sb("x1", [P, NT, F], F32)
        g.x1_one = sb("x1_one", [P, NT * F], F32)
        g.tau = sb("tau", [P, NT * KH], F32)
        g.w_exp = sb("w_exp", [P, NT * KH], F32)
        between(nc, g)
        g.u_sb = sb("u1_sb", [P, PAIRS, IB1], F32)
        g.sums_stored = sem("sums_stored")
        layer1(nc, g)
        final(nc, g)


class Chain:

    def __init__(self, eng, semaphore):
        self.eng, self.semaphore, self.count = eng, semaphore, 0

    def __call__(self, instruction):
        self.count += 1
        instruction.then_inc(self.semaphore, 1)
        self.eng.wait_ge(self.semaphore, self.count)


def over_rows(ap, shape):
    return ap.unsqueeze(1).to_broadcast(shape)


def over_columns(ap, shape):
    return ap.unsqueeze(2).to_broadcast(shape)


def row_groups(wide):
    tiles = 8 if 8 * wide <= P else 1
    return tiles, NT * P // (tiles * BANK)


def store_rows(eng, dst, rows, wide, stored):
    tiles, groups = row_groups(wide)
    by_tile = dst[0:wide, :].rearrange("k (m t i) -> t k m i", t=tiles, i=P)
    for t in range(tiles):
        src = rows[t * wide:(t + 1) * wide, 0:groups * BANK].rearrange("k (m i) -> k m i", i=P)
        eng.dma_start(by_tile[t], src).then_inc(stored, 16)


def load_adj(sp, g, b, u):
    rows = g.adj[bass.ds(b * IB0, IB0), u * UNIT:(u + 1) * UNIT]
    sp.dma_start(g.raw[:, u % RAW, :, :], rows.rearrange("(t p) j -> p t j", p=P)).then_inc(g.raw_loaded[u % RAW], 16)


def either(eng, g, program):
    flag = eng.value_load(g.general[0:1, 0:1], min_val=0, max_val=1)
    with eng.If(flag != 0):
        program(KINDS)
    with eng.Else():
        program(2)


def prepare(nc, g):
    sem = g.sem
    tau0, x0_w, r0_bc = g.tau0, g.x0_w, g.r0_bc
    small_loaded, x_loaded, xT_loaded = sem("small_loaded"), sem("x_loaded"), sem("xT_loaded")
    w0_loaded = sem("w0_loaded")
    w_loaded, consts = sem("weights_loaded"), sem("consts_ready")
    dve_step = sem("prep_dve_step")
    a_spread, pe_wa, wa_copied = sem("a_spread"), sem("pe_wa"), sem("wa_copied")
    pe_f1, f1_taken, r_made = sem("pe_f1"), sem("f1_taken"), sem("r_made")
    f2_ready, pe_maxT, max_row, pe_beta = sem("f2_ready"), sem("pe_maxT"), sem("max_row"), sem("pe_beta")
    expo_ready, exps_done = sem("expo_ready"), sem("exps_done")
    xsum_made, xsum_spread, pe_hsum = sem("xsum_made"), sem("xsum_spread"), sem("pe_hsum")
    fold_in, pe_fold = sem("fold_in"), sem("pe_fold")
    NP = H // 2
    F1_BANKS = 4
    F1_FIRST = 2
    VP_AT = 2 * TYPES * H
    BIAS_AT = VP_AT + NP * F
    with ExitStack() as local:
        xT_sb = g.sb("xT_sb", [F, N], F32, local)
        w0T_sb = g.sb("w0T_sb", [F, F], F32, local)
        a12_sb = g.sb("a12_sb", [F, 2], F32, local)
        a_wide = g.sb("a_wide", [F, 2, P], F32, local)
        wa1 = g.sb("wa1", [F, P], F32, local)
        x_wa2 = g.sb("x_wa2", [P, NT, F], F32, local)
        f2 = g.sb("f2", [P, NT], F32, local)
        f2_max = g.sb("f2_max", [P, 1], F32, local)
        beta1 = g.sb("beta1", [1, 1], F32, local)
        beta = g.sb("beta", [P, 1], F32, local)
        expo = g.sb("expo", [P, NT], F32, local)
        w_0 = g.sb("w_0", [P, NT], F32, local)
        x_copy = g.sb("x_copy", [F, N], F32, local)
        x_total = g.sb("x_total", [F, 1], F32, local)
        qk = g.sb("qk", [P, 2, DC, F + 1], F32, local)
        qk_d = g.sb("qk_d", [P, 2 * DC, P], F32, local)
        a_sb = g.sb("a_sb", [P, 2 * DC, TYPES * H], F32, local)
        vwT_sb = g.sb("vwT_sb", [F, H, F], F32, local)
        vwT_d = g.sb("vwT_d", [F, H, F], F32, local)
        vb_sb = g.sb("vb_sb", [F, H], F32, local)
        vb_bc = g.sb("vb_bc", [F, H, P], F32, local)
        pw_sb = g.sb("pw_sb", [F, H, F], F32, local)
        pb_sb = g.sb("pb_sb", [1, F], F32, local)
        xsum = g.sb("xsum", [F, P], F32, local)
        ps = [local.enter_context(nc.psum_tensor(f"prep_ps{i}", [P, BANK], F32))[:] for i in range(8)]
        block = local.enter_context(nc.Block())
        first_inputs = ((w0T_sb[:], g.w0T, small_loaded), (a12_sb[:], g.a12, small_loaded),
                        (g.x_sb[:], g.x.rearrange("(t p) c -> p t c", p=P), x_loaded),
                        (xT_sb[:], g.xT, xT_loaded),
                        (g.w0_twice[0:F, :], g.w0, w0_loaded), (g.w0_twice[F:2 * F, :], g.w0, w0_loaded))
        weights = ((qk[:, 0, :, 0:F], g.qwT.rearrange("(d p) c -> p d c", p=P)),
                   (qk[:, 1, :, 0:F], g.kwT.rearrange("(d p) c -> p d c", p=P)),
                   (qk[:, 0, :, F:F + 1], g.qb.rearrange("(d p o) -> p d o", p=P, o=1)),
                   (qk[:, 1, :, F:F + 1], g.kb.rearrange("(d p o) -> p d o", p=P, o=1)),
                   (a_sb[:], g.a_cat.rearrange("(d p) c -> p d c", p=P)),
                   (vwT_sb[:], g.vwT.rearrange("(h d) c -> d h c", d=F)),
                   (vb_sb[:], g.vb.rearrange("(h d) -> d h", d=F)),
                   (pw_sb[:], g.pw.rearrange("(h d) c -> d h c", d=F)),
                   (pb_sb[:], g.pb.rearrange("(o c) -> o c", o=1)))

        @block.sync
        def _(sp):
            for dst, src, done in first_inputs:
                sp.dma_start(dst, src).then_inc(done, 16)
            sp.wait_ge(w_loaded, 16 * len(weights))
            for u in range(RAW):
                load_adj(sp, g, 0, u)

        @block.gpsimd
        def _(pool):
            pool.memset(g.ident[:], 0.0).then_inc(consts, 1)
            pool.memset(g.ident_b[:], 0.0).then_inc(consts, 1)
            pool.wait_ge(consts, 2)
            for m in (g.ident, g.ident_b):
                pool.affine_select(out=m[:], in_=m[:], compare_op=ALU.not_equal, fill=1.0, base=0,
                                   pattern=[[-1, P]], channel_multiplier=1).then_inc(consts, 1)
            pool.memset(g.ones[:], 1.0).then_inc(consts, 1)
            pool.memset(g.minus_half[:], -0.5).then_inc(consts, 1)
            for k in range(KINDS):
                code = k if k < TYPES else -1
                pool.memset(g.neg_kind[:, k:k + 1], float(-code)).then_inc(consts, 1)

        CONSTS = 6 + KINDS

        @block.scalar
        def _(act):
            with nc.allow_non_contiguous_dma(reason="biases of one column"):
                for dst, src in weights:
                    act.dma_start(dst, src).then_inc(w_loaded, 16)
            act.wait_ge(xT_loaded, 16)
            nc.scalar.activation(x_copy[:], xT_sb[:], ACT.Copy, accum_out=x_total[:]).then_inc(xsum_made, 1)
            act.wait_ge(expo_ready, 1)
            nc.scalar.activation(w_0[:], expo[:], ACT.Exp).then_inc(exps_done, 1)
            nc.scalar.activation(tau0[:], expo[:], ACT.Exp, scale=-(1.0 - SLOPE0)).then_inc(exps_done, 1)
            for n in range(N // BANK):
                act.wait_ge(f1_taken, n + 1)
                row = r0_bc[:, n * BANK:(n + 1) * BANK]
                nc.scalar.activation(row, row, ACT.Exp, scale=1.0 - SLOPE0).then_inc(r_made, 1)

        @block.vector
        def _(dve):
            step = Chain(dve, dve_step)
            step(nc.vector.memset(g.vp_fold[:], 0.0))
            step(nc.vector.memset(g.g_fold[:], 0.0))
            dve.wait_ge(small_loaded, 32)
            nc.vector.tensor_copy(a_wide[:], over_columns(a12_sb[:], [F, 2, P])).then_inc(a_spread, 1)
            dve.wait_ge(pe_wa, 1)
            nc.vector.tensor_copy(wa1[:], ps[0][0:F, 0:P]).then_inc(wa_copied, 1)
            dve.wait_ge(x_loaded, 16)
            step(nc.vector.tensor_tensor(x_wa2[:], g.x_sb[:], over_rows(ps[0][:, P:P + F], [P, NT, F]), ALU.mult))
            step(nc.vector.tensor_reduce(f2[:], x_wa2[:], AX.X, ALU.add))
            nc.vector.tensor_reduce(f2_max[:], f2[:], AX.X, ALU.max).then_inc(f2_ready, 1)
            dve.wait_ge(consts, CONSTS)
            dve.wait_ge(w_loaded, 16 * len(weights))
            for h in range(H):
                nc.vector.tensor_scalar(vwT_d[:, h, :], vwT_sb[:, h, :], vwT_sb[:, h, F - 1:F], None,
                                        ALU.subtract).then_inc(fold_in, 1)
            qk_m = qk[:].rearrange("p s d c -> p (s d) c")
            for s in range(2):
                cols = slice(s * F, (s + 1) * F - 1)
                nc.vector.tensor_tensor(qk_d[:, :, cols], qk_m[:, :, 0:F - 1],
                                        qk_m[:, :, F - 1:F].to_broadcast([P, 2 * DC, F - 1]),
                                        ALU.subtract).then_inc(fold_in, 1)
                nc.vector.tensor_copy(qk_d[:, :, (s + 1) * F - 1:(s + 1) * F],
                                      qk_m[:, :, F:F + 1]).then_inc(fold_in, 1)
            nc.vector.tensor_tensor(vb_bc[:], over_columns(vb_sb[:], [F, H, P]),
                                    over_rows(g.ones[0:F, :], [F, H, P]), ALU.mult).then_inc(fold_in, 1)
            dve.wait_ge(pe_maxT, 1)
            nc.vector.tensor_reduce(beta1[:], ps[5][0:1, 0:P], AX.X, ALU.max).then_inc(max_row, 1)
            dve.wait_ge(pe_beta, 1)
            step(nc.vector.tensor_copy(beta[:], ps[5][:, P:P + 1]))
            nc.vector.tensor_scalar(expo[:], f2[:], beta[:], -LIMIT, ALU.subtract, ALU.max).then_inc(expo_ready, 1)
            for n in range(N // BANK):
                dve.wait_ge(pe_f1, n + 1)
                nc.vector.tensor_scalar(r0_bc[:, n * BANK:(n + 1) * BANK], ps[1 + n % F1_BANKS], beta[:],
                                        LIMIT / (1.0 - SLOPE0), ALU.add, ALU.min).then_inc(f1_taken, 1)
            dve.wait_ge(exps_done, 2)
            step(nc.vector.tensor_tensor(x0_w[:], g.x_sb[:], over_columns(w_0[:], [P, NT, F]), ALU.mult))
            step(nc.vector.tensor_copy(g.w0_rep[:], over_columns(w_0[:], [P, NT, 32])))
            step(nc.vector.tensor_reduce(g.den_rows[:], g.ident[:, 0:P:32], AX.X, ALU.add))
            dve.wait_ge(xsum_made, 1)
            nc.vector.tensor_scalar(xsum[:], g.ones[0:F, :], x_total[:], None, ALU.mult).then_inc(xsum_spread, 1)
            dve.wait_ge(pe_hsum, 1)
            step(nc.vector.tensor_copy(g.hsum[:], ps[6][:, 0:F]))
            dve.wait_ge(pe_fold, 1)
            step(nc.vector.tensor_copy(g.g_fold[:, 0:TYPES * H], ps[7][:, 0:TYPES * H]))
            step(nc.vector.tensor_copy(g.g_fold[:, KH:KH + TYPES * H], ps[7][:, TYPES * H:2 * TYPES * H]))
            for s in range(2):
                rows = slice(s * F, (s + 1) * F)
                step(nc.vector.tensor_copy(g.vp_fold[rows, :, s * F:(s + 1) * F],
                                           ps[7][rows, VP_AT:VP_AT + NP * F].rearrange("p (q c) -> p q c", q=NP)))
                step(nc.vector.tensor_copy(
                    g.vp_fold[rows, :, 2 * F + s:2 * F + s + 1],
                    over_rows(g.ident[rows, (s + 1) * F - 1:(s + 1) * F], [F, NP, 1])))
            step(nc.vector.tensor_copy(g.out_bias[:], ps[7][:, BIAS_AT:BIAS_AT + F]))

        @block.tensor
        def _(pe):
            pe.wait_ge(small_loaded, 32)
            pe.wait_ge(a_spread, 1)
            nc.tensor.matmul(ps[0][0:F, 0:P], w0T_sb[:], a_wide[:, 0, :], start=True, stop=True)
            nc.tensor.matmul(ps[0][:, P:P + F], a_wide[:, 1, :], w0T_sb[:], start=True, stop=True).then_inc(pe_wa, 1)

            def f1_row(n):
                if n >= F1_BANKS:
                    pe.wait_ge(f1_taken, n - F1_BANKS + 1)
                nc.tensor.matmul(ps[1 + n % F1_BANKS], wa1[:], xT_sb[:, n * BANK:(n + 1) * BANK], start=True,
                                 stop=True).then_inc(pe_f1, 1)

            pe.wait_ge(wa_copied, 1)
            pe.wait_ge(xT_loaded, 16)
            for n in range(F1_FIRST):
                f1_row(n)
            pe.wait_ge(consts, CONSTS)
            pe.wait_ge(f2_ready, 1)
            nc.tensor.transpose(ps[5][0:1, 0:P], f2_max[:], g.ident[:]).then_inc(pe_maxT, 1)
            pe.wait_ge(max_row, 1)
            nc.tensor.matmul(ps[5][:, P:P + 1], g.ones[0:1, :], beta1[:], start=True, stop=True).then_inc(pe_beta, 1)
            for n in range(F1_FIRST, N // BANK):
                f1_row(n)
            pe.wait_ge(w_loaded, 16 * len(weights))
            pe.wait_ge(fold_in, H + 5)
            for s in range(2):
                for d in range(DC):
                    nc.tensor.matmul(ps[7][:, s * TYPES * H:(s + 1) * TYPES * H], qk_d[:, s * DC + d, :],
                                     a_sb[:, s * DC + d, :], start=(d == 0), stop=(d == DC - 1))
            for h in range(H):
                rows = slice((h % 2) * F, (h % 2 + 1) * F)
                at = VP_AT + (h // 2) * F
                nc.tensor.matmul(ps[7][rows, at:at + F], vwT_d[:, h, :], pw_sb[:, h, :], start=True, stop=True)
            nc.tensor.matmul(ps[7][:, BIAS_AT:BIAS_AT + F], g.ones[0:1, :], pb_sb[:], start=True, stop=False)
            for h in range(H):
                last = nc.tensor.matmul(ps[7][:, BIAS_AT:BIAS_AT + F], vb_bc[:, h, :], pw_sb[:, h, :], start=False,
                                        stop=(h == H - 1))
            last.then_inc(pe_fold, 1)
            pe.wait_ge(w0_loaded, 32)
            pe.wait_ge(xsum_spread, 1)
            nc.tensor.matmul(ps[6][:, 0:F], xsum[:], g.w0_twice[0:F, :], start=True, stop=True).then_inc(pe_hsum, 1)


def layer0(nc, g):
    sem = g.sem
    code_ready = sem("code_ready")
    squared = sem("squared")
    transposed = sem("transposed")
    dense_ready = sem("dense_ready")
    t_ready = sem("t0_ready")
    multiplied = sem("multiplied")
    codes_out = sem("codes_out")
    codes_stored = [sem(f"codes_stored{n}") for n in range(2)]
    cap_ready = sem("cap_ready")
    u_copied = sem("u_copied")
    CREDIT = 4
    T_CREDIT = 2 * HALF_J
    DENSE = 2 * HALF_J - sum(CAPPED)
    with ExitStack() as local:
        code = g.sb("code", [P, 2, IT0, UNIT], BF16, local)
        junk = g.sb("junk", [P, 2, IT0 // 2 * UNIT], BF16, local)
        dense = g.sb("dense", [P, HALF_J, IB0], F32, local)
        t0 = g.sb("t0", [P, 2, HALF_J, IB0], F32, local)
        code_t = g.sb("code_t", [P, 2, HALF_J, IB0], I8, local)
        cap = g.sb("cap", [P, IB0], BF16, local)
        tp = local.enter_context(nc.psum_tensor("tp", [P, 2, HALF_J, IB0], BF16))
        u_ps = local.enter_context(nc.psum_tensor("u_ps", [P, 2, IB0], F32))
        block = local.enter_context(nc.Block())

        @block.sync
        def _(sp):
            def load_block(b, first):
                for u in range(first, UNITS):
                    sp.wait_ge(code_ready, b * UNITS + (u + 1 - RAW))
                    load_adj(sp, g, b, u)

            load_block(0, RAW)
            with sp.Fori(1, NB0) as b:
                load_block(b, 0)

        @block.vector
        def _(dve):
            dve.sem_inc(t_ready, T_CREDIT)

            def clip(b, u):
                unit = b * UNITS + u
                dve.wait_ge(g.raw_loaded[u % RAW], b * (16 * UNITS // RAW) + 16 * (u // RAW + 1))
                dve.wait_ge(squared, 2 * unit + 2)
                dve.wait_ge(transposed, 2 * unit + 2)
                nc.vector.tensor_scalar(code[:, u % 2, :, :].rearrange("p t j -> p (t j)"),
                                        g.raw[:, u % RAW, :, :].rearrange("p t j -> p (t j)"),
                                        float(TYPES - 1), -1.0, ALU.min, ALU.max).then_inc(code_ready, 1)

            def block_of_targets(b, last_block):
                for u in range(UNITS):
                    unit = b * UNITS + u
                    for n in range(2):
                        half = (b * UNITS + u) * 2 + n
                        row = g.r0_bc[:, bass.ds(b * IB0, IB0)]
                        by_code = HALF_J - CAPPED[n]
                        for a in range(by_code):
                            jt = (u * 2 + n) * HALF_J + a
                            dve.wait_ge(t_ready, half * HALF_J + (T_CREDIT - HALF_J + a + 1))
                            nc.vector.tensor_scalar(dense[:, a, :], row, g.tau0[:, jt:jt + 1], None,
                                                    ALU.max).then_inc(dense_ready, 1)
                        dve.wait_ge(codes_out, half + 1)
                        dve.wait_ge(multiplied, half + 1)
                        for a in range(by_code):
                            dve.wait_ge(dense_ready, unit * DENSE + n * (HALF_J - CAPPED[0]) + a + 1)
                            nc.vector.scalar_tensor_tensor(t0[:, n, a, :], code_t[:, n, a, :], 0.0, dense[:, a, :],
                                                           ALU.is_gt, ALU.mult).then_inc(t_ready, 1)
                        if CAPPED[n]:
                            jt = (u * 2 + n) * HALF_J + by_code
                            dve.wait_ge(cap_ready, unit + 1)
                            nc.vector.scalar_tensor_tensor(t0[:, n, by_code, :], row, g.tau0[:, jt:jt + 1], cap[:],
                                                           ALU.max, ALU.min).then_inc(t_ready, 1)
                        if n == 0 and u + 1 < UNITS:
                            clip(b, u + 1)
                        elif n == 0 and not last_block:
                            clip(b + 1, 0)

            clip(0, 0)
            with dve.Fori(0, NB0 - 1) as b:
                block_of_targets(b, False)
            block_of_targets(NB0 - 1, True)

        @block.scalar
        def _(act):
            act.sem_inc(squared, 4)
            for n in range(2):
                act.sem_inc(codes_stored[n], 16)

            def take_codes(b, u, n):
                unit = b * UNITS + u
                half = unit * 2 + n
                act.wait_ge(transposed, half + 1 + CREDIT)
                act.wait_ge(codes_stored[n], 16 * unit + 16)
                act.wait_ge(t_ready, half * HALF_J + HALF_J)
                nc.scalar.activation(code_t[:, n, :, :].rearrange("p a i -> p (a i)"),
                                     tp[:, n, :, :].rearrange("p a i -> p (a i)"), ACT.Copy).then_inc(codes_out, 1)
                if CAPPED[n]:
                    nc.scalar.activation(cap[:], tp[:, n, HALF_J - 1, :], ACT.Relu,
                                         scale=CAP).then_inc(cap_ready, 1)

            def store_codes(b, u, n):
                unit = b * UNITS + u
                half = unit * 2 + n
                rows = slice(n * IT0 // 2, (n + 1) * IT0 // 2)
                nc.scalar.activation(junk[:, n, :], code[:, u % 2, rows, :].rearrange("p t j -> p (t j)"),
                                     ACT.Square, bias=g.minus_half[:],
                                     accum_out=g.off_sum[:, bass.ds(half, 1)]).then_inc(squared, 1)
                act.wait_ge(codes_out, half + 1)
                rows = (u * 2 + n) * HALF_J * P
                dst = g.codes_dram[rows:rows + HALF_J * P, bass.ds(b * IB0, IB0)]
                act.dma_start(dst.rearrange("(a p) i -> p a i", p=P), code_t[:, n, :, :]).then_inc(codes_stored[n], 16)

            def block_of_targets(b, last_block):
                for u in range(UNITS):
                    for n in range(2):
                        if (u, n) != (0, 0):
                            take_codes(b, u, n)
                            store_codes(b, u, n)
                if not last_block:
                    take_codes(b + 1, 0, 0)
                act.wait_ge(multiplied, b * HALVES + HALVES + 2)
                for s in range(2):
                    nc.scalar.activation(g.u_all[:, s, bass.ds(b * IB0, IB0)], u_ps[:, s, :],
                                         ACT.Copy).then_inc(u_copied, 1)
                if not last_block:
                    store_codes(b + 1, 0, 0)

            take_codes(0, 0, 0)
            store_codes(0, 0, 0)
            with act.Fori(0, NB0 - 1) as b:
                block_of_targets(b, False)
            block_of_targets(NB0 - 1, True)
            for n in range(2):
                act.wait_ge(codes_stored[n], 16 * (NB0 * UNITS + 1))

        @block.tensor
        def _(pe):
            pe.sem_inc(transposed, CREDIT)
            pe.sem_inc(multiplied, 2)

            def transpose(b, u, n):
                half = (b * UNITS + u) * 2 + n
                if n == 0:
                    pe.wait_ge(code_ready, b * UNITS + u + 1)
                if not isinstance(half, int) or half >= 2:
                    pe.wait_ge(codes_out, half - 1)
                    if CAPPED[n]:
                        pe.wait_ge(cap_ready, b * UNITS + u)
                for a in range(HALF_J):
                    for t in range(IT0):
                        j = (n * HALF_J + a) * P
                        last = nc.tensor.transpose(tp[:, n, a, t * P:(t + 1) * P], code[:, u % 2, t, j:j + P],
                                                   g.ident_b[:])
                last.then_inc(transposed, 1)

            def add_numerators(b, u, n):
                half = (b * UNITS + u) * 2 + n
                if u == 0 and n == 0 and (not isinstance(b, int) or b >= 1):
                    pe.wait_ge(u_copied, 2 * b)
                pe.wait_ge(t_ready, half * HALF_J + (T_CREDIT + HALF_J))
                jt = (u * 2 + n) * HALF_J
                for c in range(0, IB0, BANK):
                    for a in range(HALF_J):
                        nc.tensor.matmul(u_ps[a * F:(a + 1) * F, 0, c:c + BANK], g.x0_w[:, jt + a, :],
                                         t0[:, n, a, c:c + BANK], start=(jt == 0), stop=(jt == NT - HALF_J))

            def add_denominators(b, u, n):
                jt = (u * 2 + n) * HALF_J
                for c in range(0, IB0, BANK):
                    for a in range(HALF_J):
                        r = (jt + a) % 4 * 32
                        last = nc.tensor.matmul(u_ps[r:r + 32, 1, c:c + BANK], g.w0_rep[:, jt + a, :],
                                                t0[:, n, a, c:c + BANK], start=(jt < 4), stop=(jt >= NT - 4))
                last.then_inc(multiplied, 1)

            order = [(u, n) for u in range(UNITS) for n in range(2)]

            def block_of_targets(b, last_block):
                for m, (u, n) in enumerate(order):
                    add_numerators(b, u, n)
                    if m + 2 < HALVES:
                        transpose(b, *order[m + 2])
                    elif not last_block:
                        transpose(b + 1, 0, n)
                    add_denominators(b, u, n)

            transpose(0, 0, 0)
            transpose(0, 0, 1)
            block_of_targets(0, False)
            with pe.Fori(1, NB0 - 1) as b:
                block_of_targets(b, False)
            block_of_targets(NB0 - 1, True)


def between(nc, g):
    sem = g.sem
    dve_step, tables_step = sem("between_dve_step"), sem("tables_dve_step")
    elu_in, elu_exp = sem("elu_in"), sem("elu_exp")
    centered, squares, var_ready, root = sem("centered0"), sem("squares0"), sem("var0"), sem("root0")
    ones_set = sem("ones_set")
    x1_ready, xT_made, xT_copied = sem("x1_ready"), sem("x1T_made"), sem("x1T_copied")
    s_made, s_copied = sem("s_made"), sem("s_copied")
    max_ready, max_made, beta_diag, beta_made = sem("b_max"), sem("b_maxT"), sem("beta_diag"), sem("beta_made")
    expo_ready, exps_done = sem("expo1_ready"), sem("exps1_done")
    rows_made, rows_copied = sem("rows_made"), sem("rows_copied")
    flag_max, flag_row = sem("flag_max"), sem("flag_row")
    den_made, num_made = sem("den_made"), sem("num_made")
    TG = BANK // P
    BANKS = 7
    with ExitStack() as local:
        z = g.sb("z", [P, NT], F32, local)
        den = g.sb("den", [P, NT], F32, local)
        rec = g.sb("rec", [P, NT], F32, local)
        ha = g.sb("ha", [P, NT, F], F32, local)
        hb = g.sb("hb", [P, NT, F], F32, local)
        x1T = g.sb("x1T", [P, N // 2], F32, local)
        s12_all = g.sb("s12", [P, NT * 2 * KH], F32, local)
        b_max = g.sb("b_max", [P, KH], F32, local)
        beta_col = g.sb("beta_col", [KH, 1], F32, local)
        beta_d = g.sb("beta_d", [KH, KH], F32, local)
        beta_r = g.sb("beta_r", [P, KH], F32, local)
        e_r_all = g.sb("e_r", [P, NT * KH], F32, local)
        e_t_all = g.sb("e_t", [P, NT * KH], F32, local)
        e_c_all = g.sb("e_c", [P, NT * KH], F32, local)
        m_max = g.sb("m_max", [P, NT, H], F32, local)
        rowsT = g.u_all
        off_max = g.sb("off_max", [P, 1], F32, local)
        off_row = g.sb("off_row", [1, 1], F32, local)
        ps_all = local.enter_context(nc.psum_tensor("mid_ps", [P, 8, BANK], F32))
        ps = [ps_all[:, i, :] for i in range(8)]
        NTM = NT // 2
        num_banks = NT * F // BANK
        num0 = ps_all[:, 0:num_banks, :].rearrange("p n (t c) -> p (n t) c", c=F)
        den0 = [ps_all[:, num_banks + m, 0:NTM] for m in range(2)]
        block = local.enter_context(nc.Block())

        x1_one = g.x1_one[:].rearrange("p (t c) -> p t c", c=F)

        def tiles_of(m):
            return slice(m * NTM, (m + 1) * NTM)

        def tables(kinds):
            wide = kinds * H

            def table(ap):
                return ap[:, 0:NT * wide].rearrange("p (t c) -> p t c", c=wide)

            s12 = s12_all[:, 0:NT * 2 * wide].rearrange("p (t s c) -> p t s c", s=2, c=wide)
            return wide, s12, table(e_r_all), table(e_t_all), table(e_c_all)

        def score_groups(wide):
            tiles = min(BANK // (2 * wide), 8)
            return [(odd, t, min(tiles, NT // 2 - t)) for t in range(0, NT // 2, tiles) for odd in range(2)]

        @block.gpsimd
        def _(pool):
            pool.memset(x1_one[:, :, F - 1:F], 1.0).then_inc(ones_set, 1)

        @block.vector
        def _(dve):
            step = Chain(dve, dve_step)
            nc.vector.tensor_reduce(off_max[:], g.off_sum[:], AX.X, ALU.max).then_inc(flag_max, 1)
            def divide_in(m):
                t, shape = tiles_of(m), [P, NTM, F]
                dve.wait_ge(den_made, m + 1)
                step(nc.vector.tensor_scalar(z[:, t], den0[m], 0.0, None, ALU.is_equal))
                step(nc.vector.scalar_tensor_tensor(den[:, t], z[:, t], float(N), den0[m], ALU.mult, ALU.add))
                step(nc.vector.reciprocal(rec[:, t], den[:, t]))
                step(nc.vector.tensor_tensor(ha[:, t, :], over_rows(g.hsum[:], shape), over_columns(z[:, t], shape),
                                             ALU.mult))

            def divide(m):
                t, shape = tiles_of(m), [P, NTM, F]
                dve.wait_ge(num_made, m + 1)
                step(nc.vector.tensor_tensor(ha[:, t, :], ha[:, t, :], num0[:, t, :], ALU.add))
                nc.vector.tensor_tensor(ha[:, t, :], ha[:, t, :], over_columns(rec[:, t], shape),
                                        ALU.mult).then_inc(elu_in, 1)

            def residual(m):
                t, shape = tiles_of(m), [P, NTM, F]
                dve.wait_ge(elu_exp, 2 * m + 1)
                step(nc.vector.scalar_tensor_tensor(ha[:, t, :], ha[:, t, :], 0.0, g.x_sb[:, t, :], ALU.max, ALU.add))
                dve.wait_ge(elu_exp, 2 * m + 2)
                step(nc.vector.scalar_tensor_tensor(ha[:, t, :], hb[:, t, :], -1.0, ha[:, t, :], ALU.add, ALU.add))
                step(nc.vector.tensor_reduce(z[:, t], ha[:, t, :], AX.X, ALU.add))
                step(nc.vector.tensor_scalar(z[:, t], z[:, t], 1.0 / F, None, ALU.mult))
                nc.vector.tensor_tensor(ha[:, t, :], ha[:, t, :], over_columns(z[:, t], shape),
                                        ALU.subtract).then_inc(centered, 1)

            def variance(m):
                t = tiles_of(m)
                dve.wait_ge(squares, m + 1)
                step(nc.vector.tensor_reduce(den[:, t], hb[:, t, :], AX.X, ALU.add))
                nc.vector.tensor_scalar(den[:, t], den[:, t], 1.0 / F, EPS, ALU.mult, ALU.add).then_inc(var_ready, 1)

            def scale(m):
                t = tiles_of(m)
                dve.wait_ge(root, m + 1)
                step(nc.vector.reciprocal(rec[:, t], rec[:, t]))
                nc.vector.tensor_tensor(x1_one[:, t, 0:F - 1], ha[:, t, 0:F - 1],
                                        over_columns(rec[:, t], [P, NTM, F - 1]), ALU.mult).then_inc(x1_ready, 1)

            divide_in(0)
            step(nc.vector.tensor_reduce(off_row[:], ps[7][0:1, BANK - P:BANK], AX.X, ALU.max))
            quiet = float(IT0 // 2 * UNIT) / 4.0
            nc.vector.tensor_scalar(g.general[:], off_row[:], quiet, None, ALU.is_gt).then_inc(flag_row, 1)
            divide(0)
            residual(0)
            divide_in(1)
            variance(0)
            divide(1)
            scale(0)
            residual(1)
            variance(1)
            scale(1)
            step(nc.vector.tensor_tensor(g.x1[:], ha[:], over_columns(rec[:], [P, NT, F]), ALU.mult))
            for n in range(NT // 2 // TG):
                dve.wait_ge(xT_made, n + 1)
                nc.vector.tensor_copy(x1T[:, n * BANK:(n + 1) * BANK], ps[n]).then_inc(xT_copied, 1)
            dve.wait_ge(flag_row, 1)

            def program(kinds):
                step = Chain(dve, tables_step)
                wide, s12, e_r, e_t, e_c = tables(kinds)
                by_parity = s12_all[:, 0:NT * 2 * wide].rearrange("p (t o c) -> p t o c", o=2, c=2 * wide)
                for n, (odd, first, m) in enumerate(score_groups(wide)):
                    dve.wait_ge(s_made, n + 1)
                    nc.vector.tensor_copy(by_parity[:, first:first + m, odd, :],
                                          ps[n % BANKS][:, 0:m * 2 * wide].rearrange("p (t c) -> p t c", t=m)
                                          ).then_inc(s_copied, 1)
                dve.wait_ge(s_copied, len(score_groups(wide)))
                nc.vector.tensor_reduce(b_max[:, 0:wide], s12[:, :, 1, :].rearrange("p t c -> p c t"), AX.X,
                                        ALU.max).then_inc(max_ready, 1)
                dve.wait_ge(max_made, 1)
                step(nc.vector.tensor_reduce(beta_col[0:wide, :], ps[7][0:wide, 0:P], AX.X, ALU.max))
                nc.vector.tensor_scalar(beta_d[0:wide, 0:wide], g.ident[0:wide, 0:wide], beta_col[0:wide, :], None,
                                        ALU.mult).then_inc(beta_diag, 1)
                dve.wait_ge(beta_made, 1)
                step(nc.vector.tensor_copy(beta_r[:, 0:wide], ps[7][:, P:P + wide]))
                shape = [P, NT, wide]
                step(nc.vector.tensor_tensor(e_r, s12[:, :, 0, :], over_rows(beta_r[:, 0:wide], shape), ALU.add))
                step(nc.vector.scalar_tensor_tensor(e_c, e_r, SLOPE1, e_r, ALU.mult, ALU.max))
                step(nc.vector.tensor_scalar(e_r, e_r, 1.0 - SLOPE1, LIMIT, ALU.mult, ALU.min))
                step(nc.vector.tensor_tensor(e_t, s12[:, :, 1, :], over_rows(beta_r[:, 0:wide], shape),
                                             ALU.subtract))
                nc.vector.tensor_scalar(e_t, e_t, -LIMIT, None, ALU.max).then_inc(expo_ready, 1)
                step(nc.vector.tensor_reduce(m_max[:], e_c.rearrange("p t (k h) -> p t h k", h=H), AX.X, ALU.max))
                for k in range(kinds):
                    cols = slice(k * H, (k + 1) * H)
                    step(nc.vector.tensor_tensor(e_c[:, :, cols], e_c[:, :, cols], m_max[:], ALU.subtract))
                step(nc.vector.tensor_scalar(s12[:, :, 0, :], e_r, 0.0, None, ALU.max))
                nc.vector.tensor_tensor(e_c, e_c, s12[:, :, 0, :], ALU.subtract).then_inc(expo_ready, 1)
                tiles, groups = row_groups(wide)
                for n in range(2 * groups):
                    s, m = divmod(n, groups)
                    dve.wait_ge(rows_made, n + 1)
                    nc.vector.tensor_copy(rowsT[0:tiles * wide, s, m * BANK:(m + 1) * BANK],
                                          ps[n % BANKS][0:tiles * wide, :]).then_inc(rows_copied, 1)

            either(dve, g, program)

        @block.scalar
        def _(act):
            for m in range(2):
                t = tiles_of(m)
                act.wait_ge(elu_in, m + 1)
                nc.scalar.activation(hb[:, t, :], ha[:, t, :], ACT.Relu, scale=-1.0).then_inc(elu_exp, 1)
                act.wait_ge(elu_exp, 2 * m + 1)
                nc.scalar.activation(hb[:, t, :], hb[:, t, :], ACT.Exp, scale=-1.0).then_inc(elu_exp, 1)
                act.wait_ge(centered, m + 1)
                nc.scalar.activation(hb[:, t, :], ha[:, t, :], ACT.Square).then_inc(squares, 1)
                act.wait_ge(var_ready, m + 1)
                nc.scalar.activation(rec[:, t], den[:, t], ACT.Sqrt).then_inc(root, 1)
            act.wait_ge(flag_row, 1)

            def program(kinds):
                wide, s12, e_r, e_t, e_c = tables(kinds)
                act.wait_ge(expo_ready, 1)
                nc.scalar.activation(g.tau[:, 0:NT * wide], e_t_all[:, 0:NT * wide], ACT.Exp,
                                     scale=-(1.0 - SLOPE1)).then_inc(exps_done, 1)
                nc.scalar.activation(g.w_exp[:, 0:NT * wide], e_t_all[:, 0:NT * wide], ACT.Exp).then_inc(exps_done, 1)
                act.wait_ge(expo_ready, 2)
                nc.scalar.activation(e_r, e_r, ACT.Exp).then_inc(exps_done, 1)
                nc.scalar.activation(e_c, e_c, ACT.Exp).then_inc(exps_done, 1)

            either(act, g, program)

        @block.tensor
        def _(pe):
            pe.wait_ge(flag_max, 1)
            nc.tensor.transpose(ps[7][0:1, BANK - P:BANK], off_max[:], g.ident[:])
            for m in range(2):
                for t in range(NTM):
                    i = (m * NTM + t) * P
                    last = nc.tensor.matmul(den0[m][:, t:t + 1], g.u_all[:, 1, i:i + P], g.den_rows[:],
                                            start=True, stop=True)
                last.then_inc(den_made, 1)
                for t in range(NTM):
                    i = (m * NTM + t) * P
                    last = nc.tensor.matmul(num0[:, m * NTM + t, :], g.u_all[:, 0, i:i + P], g.w0_twice[:],
                                            start=True, stop=True)
                last.then_inc(num_made, 1)
            pe.wait_ge(ones_set, 1)
            for n in range(NT // 2 // TG):
                pe.wait_ge(x1_ready, n // (NTM // 2 // TG) + 1)
                for t in range(TG):
                    pair = n * TG + t
                    last = nc.tensor.transpose(ps[n][:, t * P:(t + 1) * P],
                                               g.x1_one[:, pair * 2 * F:(pair + 1) * 2 * F], g.ident[:])
                last.then_inc(xT_made, 1)
            pe.wait_ge(flag_row, 1)

            def program(kinds):
                wide, s12, e_r, e_t, e_c = tables(kinds)
                folded = g.g_fold[:].rearrange("c (s k) -> c s k", s=2)[:, :, 0:wide]
                pe.wait_ge(xT_copied, NT // 2 // TG)
                for n, (odd, first, m) in enumerate(score_groups(wide)):
                    if n >= BANKS:
                        pe.wait_ge(s_copied, n - BANKS + 1)
                    half = slice(odd * F, (odd + 1) * F)
                    for t in range(m):
                        last = nc.tensor.matmul(ps[n % BANKS][:, t * 2 * wide:(t + 1) * 2 * wide],
                                                x1T[half, (first + t) * P:(first + t + 1) * P], folded[half, :, :],
                                                start=True, stop=True)
                    last.then_inc(s_made, 1)
                pe.wait_ge(max_ready, 1)
                nc.tensor.transpose(ps[7][0:wide, 0:P], b_max[:, 0:wide], g.ident[:]).then_inc(max_made, 1)
                pe.wait_ge(beta_diag, 1)
                nc.tensor.matmul(ps[7][:, P:P + wide], g.ones[0:wide, :], beta_d[0:wide, 0:wide], start=True,
                                 stop=True).then_inc(beta_made, 1)
                tiles, groups = row_groups(wide)
                for n in range(2 * groups):
                    s, m = divmod(n, groups)
                    if m == 0:
                        pe.wait_ge(exps_done, 3 + s)
                    if n >= BANKS:
                        pe.wait_ge(rows_copied, n - BANKS + 1)
                    for t in range(TG):
                        c = (m * TG + t) * tiles * wide
                        last = nc.tensor.transpose(ps[n % BANKS][0:tiles * wide, t * P:(t + 1) * P],
                                                   (e_r_all, e_c_all)[s][:, c:c + tiles * wide], g.ident[:])
                    last.then_inc(rows_made, 1)

            either(pe, g, program)


def layer1(nc, g):
    sem = g.sem
    codes_loaded = [sem(f"codes_loaded{n}") for n in range(UNROLL)]
    rows_loaded = [sem(f"rows_loaded{h}") for h in range(HG)]
    factors_loaded = sem("factors_loaded")
    kind_set = sem("kind_set")
    mask_square = sem("mask_square")
    mask_ready = sem("mask_ready")
    w_ready = sem("w_ready")
    t_ready = sem("t1_ready")
    pairs_done = sem("pairs_done")
    weighed = sem("weighed")
    sums_stored, u_sb = g.sums_stored, g.u_sb
    r_stored, c_stored, bias_added = sem("r_stored"), sem("c_stored"), sem("bias_added")
    T_CREDIT = UNROLL * HG
    P_CREDIT = UNROLL * PAIRS
    FACTORS_AT = 4
    with ExitStack() as local:
        rows = g.sb("rows", [P, HG, IB1], F32, local)
        factors = g.sb("factors", [P, PAIRS, IB1], F32, local)
        t1 = g.sb("t1", [P, PAIRS, 2, IB1], F32, local)
        mask = g.sb("mask", [P, UNROLL, IB1], BF16, local)
        kind = g.sb("kind", [P, 1], F32, local)
        off_kind = g.sb("off_kind", [P, 2, IB1], I8, local)
        codes = g.sb("codes", [P, UNROLL, IB1], I8, local)
        x_w = g.sb("x_w", [P, UNROLL, HG, F], F32, local)
        u_ps = local.enter_context(nc.psum_tensor("u1_ps", [P, PAIRS, IB1], F32))
        block = local.enter_context(nc.Block())

        def passes(eng, kinds, one_pass, peel_first=False):
            def visit(v, first):
                one_pass(v, 0, v * kinds, *first)
                if kinds > 2:
                    with eng.Fori(1, kinds - 1) as k:
                        one_pass(v, k, v * kinds + k)
                one_pass(v, kinds - 1, v * kinds + (kinds - 1))

            if peel_first:
                visit(0, (True,))
                with eng.Fori(1, VISITS) as v:
                    visit(v, ())
            else:
                with eng.Fori(0, VISITS) as v:
                    visit(v, ())

        @block.sync
        def _(sp):
            def program(kinds):
                def load_codes(v, s, number):
                    b = v // GROUPS
                    for n in range(UNROLL):
                        sp.wait_ge(mask_ready, number * UNROLL + n + 1)
                        src = g.codes_dram[bass.ds((s * UNROLL + n) * P, P), bass.ds(b * IB1, IB1)]
                        sp.dma_start(codes[:, n, :], src).then_inc(codes_loaded[n], 16)

                def one_pass(v, k, p):
                    b, group = v // GROUPS, v % GROUPS
                    for h in range(HG):
                        sp.wait_ge(t_ready, p * (NT * HG) + (T_CREDIT - HG + h + 1))
                        src = g.r_dram[bass.ds(k * H + group * HG + h, 1), bass.ds(b * IB1, IB1)]
                        sp.dma_start(rows[:, h, :], src.to_broadcast([P, IB1])).then_inc(rows_loaded[h], 16)
                    with sp.Fori(1, FACTORS_AT) as s:
                        load_codes(v, s, p * STEPS + s)
                    sp.wait_ge(c_stored, row_groups(kinds * H)[0] * 16)
                    for q in range(PAIRS):
                        for s in range(2):
                            src = g.c_dram[bass.ds(k * H + group * HG + (2 * q + s), 1), bass.ds(b * IB1, IB1)]
                            sp.dma_start(factors[s * F:(s + 1) * F, q, :],
                                         src.to_broadcast([F, IB1])).then_inc(factors_loaded, 16)
                    last_kind = isinstance(k, int) and k == kinds - 1
                    with sp.Fori(FACTORS_AT, STEPS + 1) as s:
                        load_codes((v + s // STEPS) % VISITS if last_kind else v, s % STEPS, p * STEPS + s)

                load_codes(0, 0, 0)
                store_rows(sp, g.r_dram, g.u_all[:, 0, :], kinds * H, r_stored)
                sp.wait_ge(r_stored, row_groups(kinds * H)[0] * 16)
                passes(sp, kinds, one_pass)
                for n in range(UNROLL):
                    sp.wait_ge(codes_loaded[n], 16 * (VISITS * kinds * STEPS + 1))

            either(sp, g, program)

        @block.gpsimd
        def _(pool):
            def program(kinds):
                store_rows(pool, g.c_dram, g.u_all[:, 1, :], kinds * H, c_stored)
                nc.gpsimd.tensor_tensor(g.x1[:], g.x1[:], over_rows(g.out_bias[:], [P, NT, F]),
                                        ALU.add).then_inc(bias_added, 1)
                pool.wait_ge(bias_added, 1)
                for p in range(VISITS * kinds):
                    dst = g.acc_dram[p // kinds]
                    pool.wait_ge(weighed, p * PAIRS + PAIRS)
                    if p % kinds == 0:
                        pool.dma_start(dst, u_sb[:]).then_inc(sums_stored, 16)
                    else:
                        pool.wait_ge(sums_stored, p * 16)
                        pool.dma_start(dst, u_sb[:], accum_op=ALU.add,
                                       max_dma_last_dim=IB1 * 4).then_inc(sums_stored, 16)

            either(pool, g, program)

        @block.scalar
        def _(act):
            act.sem_inc(mask_ready, UNROLL)

            def program(kinds):
                wide = kinds * H

                def set_kind(k, number):
                    nc.scalar.activation(kind[:], g.neg_kind[:, bass.ds(k, 1)], ACT.Copy).then_inc(kind_set, 1)
                    act.wait_ge(kind_set, number + 1)

                def make_masks(v, k, s, number):
                    for n in range(UNROLL):
                        tile = number * UNROLL + n
                        act.wait_ge(pairs_done, tile * PAIRS + PAIRS)
                        act.wait_ge(t_ready, tile * HG + HG)
                        act.wait_ge(mask_ready, tile + (UNROLL - 1))
                        act.wait_ge(codes_loaded[n], 16 * number + 16)
                        nc.scalar.activation(off_kind[:, n % 2, :], codes[:, n, :], ACT.Square,
                                             bias=kind[:]).then_inc(mask_square, 1)
                        for h in range(HG):
                            col = (s * UNROLL + n) * wide + k * H + (v % GROUPS) * HG + h
                            last = nc.scalar.activation(x_w[:, n, h, :], g.x1_one[:, bass.ds((s * UNROLL + n) * F, F)],
                                                        ACT.Copy, scale=g.w_exp[:, bass.ds(col, 1)])
                        last.then_inc(w_ready, 1)
                        act.wait_ge(mask_square, tile + 1)
                        nc.scalar.activation(mask[:, n, :], off_kind[:, n % 2, :], ACT.Relu, bias=1.0,
                                             scale=-1.0).then_inc(mask_ready, 1)

                def one_pass(v, k, p):
                    with act.Fori(1, STEPS) as s:
                        make_masks(v, k, s, p * STEPS + s)
                    last_kind = isinstance(k, int) and k == kinds - 1
                    k_next = 0 if last_kind else k + 1
                    set_kind(k_next, p + 1)
                    make_masks(v + 1 if last_kind else v, k_next, 0, (p + 1) * STEPS)

                set_kind(0, 0)
                make_masks(0, 0, 0, 0)
                passes(act, kinds, one_pass)

            either(act, g, program)

        @block.vector
        def _(dve):
            dve.sem_inc(t_ready, T_CREDIT)

            def program(kinds):
                wide = kinds * H

                def one_pass(v, k, p, first_pass=False):
                    def step(s, first):
                        for n in range(UNROLL):
                            tile = p * NT + s * UNROLL + n
                            dve.wait_ge(mask_ready, tile + 1 + UNROLL)
                            for h in range(HG):
                                q = h // 2
                                if h % 2 == 0:
                                    dve.wait_ge(pairs_done, tile * PAIRS + (P_CREDIT - PAIRS + q + 1))
                                if first and n == 0:
                                    dve.wait_ge(rows_loaded[h], 16 * p + 16)
                                col = (s * UNROLL + n) * wide + k * H + (v % GROUPS) * HG + h
                                nc.vector.scalar_tensor_tensor(
                                    t1[:, q, h % 2, :], rows[:, h, :], g.tau[:, bass.ds(col, 1)], mask[:, n, :],
                                    ALU.max, ALU.mult).then_inc(t_ready, 1)

                    step(0, True)
                    with dve.Fori(1, STEPS) as s:
                        step(s, False)
                    dve.wait_ge(factors_loaded, (p + 1) * (16 * HG))
                    if not first_pass:
                        dve.wait_ge(sums_stored, p * 16)
                    for q in range(PAIRS):
                        dve.wait_ge(pairs_done, p * (NT * PAIRS) + (P_CREDIT + (NT - 1) * PAIRS + q + 1))
                        nc.vector.tensor_tensor(u_sb[:, q, :], u_ps[:, q, :], factors[:, q, :],
                                                ALU.mult).then_inc(weighed, 1)

                passes(dve, kinds, one_pass, peel_first=True)

            either(dve, g, program)

        @block.tensor
        def _(pe):
            pe.sem_inc(pairs_done, P_CREDIT)

            def program(kinds):
                def multiply(tile, p, n, first, last_tile):
                    pe.wait_ge(w_ready, tile + 1)
                    for q in range(PAIRS):
                        pe.wait_ge(t_ready, tile * HG + (T_CREDIT + 2 * q + 2))
                        if first and (not isinstance(p, int) or p >= 1):
                            pe.wait_ge(weighed, p * PAIRS - PAIRS + q + 1)
                        for c in range(0, IB1, BANK):
                            for s in range(2):
                                last = nc.tensor.matmul(u_ps[s * F:(s + 1) * F, q, c:c + BANK],
                                                        x_w[:, n, 2 * q + s, :], t1[:, q, s, c:c + BANK],
                                                        start=first, stop=last_tile)
                        last.then_inc(pairs_done, 1)

                def one_pass(v, k, p, first=False):
                    for n in range(UNROLL):
                        multiply(p * NT + n, p, n, n == 0, False)
                    with pe.Fori(1, STEPS - 1) as s:
                        for n in range(UNROLL):
                            multiply(p * NT + s * UNROLL + n, p, n, False, False)
                    for n in range(UNROLL):
                        multiply(p * NT + ((STEPS - 1) * UNROLL + n), p, n, False, n == UNROLL - 1)

                passes(pe, kinds, one_pass, peel_first=True)

            either(pe, g, program)


def final(nc, g):
    sem = g.sem
    LOAD = 512
    IN = 4
    ITC = 2
    CHUNKS = NT // ITC
    PER_LOAD = LOAD // (ITC * P)
    SLOTS = 2
    HP = H // 2
    WIDE = 256
    NORMS = 2
    NTN = NT // NORMS
    sums_loaded = [sem(f"sums_loaded{n}") for n in range(IN)]
    projected, divided, y_read, rden_step = sem("projected"), sem("divided"), sem("y_read"), sem("final_rden_step")
    dve_step = sem("final_dve_step")
    centered, squares, var_ready, root = sem("centered1"), sem("squares1"), sem("var1"), sem("root1")
    out_ready, out_stored = sem("out_ready"), sem("out_stored")
    with ExitStack() as local:
        sums = g.sb("sums_in", [P, IN, HP, LOAD], F32, local)
        rden = g.sb("rden", [P, SLOTS, ITC * HP, 2], F32, local)
        y = g.sb("y", [P, SLOTS, ITC, H, F], F32, local)
        o = g.sb("o", [P, NT, F], F32, local)
        sq = g.sb("sq", [P, NT, F], F32, local)
        mean = g.sb("mean", [P, NT], F32, local)
        var = g.sb("var", [P, NT], F32, local)
        rec = g.sb("rec1", [P, NT], F32, local)
        ps = local.enter_context(nc.psum_tensor("fin_ps", [P, SLOTS, ITC * HP, WIDE], F32))
        block = local.enter_context(nc.Block())
        out_tiles = g.out.rearrange("(t p) c -> p t c", p=P)

        def tiles(m):
            return slice(m * NTN, (m + 1) * NTN)

        @block.sync
        def _(sp):
            def program(kinds):
                sp.wait_ge(g.sums_stored, 16 * GROUPS * kinds)
                for n in range(N // LOAD):
                    b, i = divmod(n * LOAD, IB1)
                    if (b, i) == (1, 0):
                        sp.wait_ge(g.sums_stored, 16 * VISITS * kinds)
                    if n >= IN:
                        sp.wait_ge(projected, (n - IN + 1) * PER_LOAD)
                    for group in range(GROUPS):
                        src = g.acc_dram[b * GROUPS + group, :, :, i:i + LOAD]
                        sp.dma_start(sums[:, n % IN, group * PAIRS:(group + 1) * PAIRS, :],
                                     src).then_inc(sums_loaded[n % IN], 16)

            either(sp, g, program)
            for m in range(NORMS):
                sp.wait_ge(out_ready, m + 1)
                sp.dma_start(out_tiles[:, tiles(m), :], o[:, tiles(m), :]).then_inc(out_stored, 16)
            sp.wait_ge(out_stored, 16 * NORMS)

        @block.tensor
        def _(pe):
            for c in range(CHUNKS):
                n, slot = c // PER_LOAD, c % SLOTS
                pe.wait_ge(sums_loaded[n % IN], 16 * GROUPS * (n // IN + 1))
                if c >= SLOTS:
                    pe.wait_ge(divided, c - SLOTS + 1)
                for t in range(ITC):
                    i = (c % PER_LOAD * ITC + t) * P
                    for q in range(HP):
                        last = nc.tensor.matmul(ps[:, slot, t * HP + q, 0:2 * F + 2], sums[:, n % IN, q, i:i + P],
                                                g.vp_fold[:, q, :], start=True, stop=True)
                last.then_inc(projected, 1)

        @block.vector
        def _(dve):
            step = Chain(dve, dve_step)

            def add_heads(c):
                dve.wait_ge(divided, c + 1)
                nc.vector.tensor_reduce(o[:, c * ITC:(c + 1) * ITC, :],
                                        y[:, c % SLOTS, :, :, :].rearrange("p t h c -> p t c h"), AX.X,
                                        ALU.add).then_inc(y_read, 1)

            def center(m):
                part, shape = o[:, tiles(m), :], [P, NTN, F]
                dve.wait_ge(y_read, (m + 1) * CHUNKS // NORMS)
                step(nc.vector.tensor_tensor(part, part, g.x1[:, tiles(m), :], ALU.add))
                step(nc.vector.tensor_reduce(mean[:, tiles(m)], part, AX.X, ALU.add))
                step(nc.vector.tensor_scalar(mean[:, tiles(m)], mean[:, tiles(m)], 1.0 / F, None, ALU.mult))
                nc.vector.tensor_tensor(part, part, over_columns(mean[:, tiles(m)], shape),
                                        ALU.subtract).then_inc(centered, 1)

            def variance(m):
                dve.wait_ge(squares, m + 1)
                step(nc.vector.tensor_reduce(var[:, tiles(m)], sq[:, tiles(m), :], AX.X, ALU.add))
                nc.vector.tensor_scalar(var[:, tiles(m)], var[:, tiles(m)], 1.0 / F, EPS, ALU.mult,
                                        ALU.add).then_inc(var_ready, 1)

            def scale(m):
                part = o[:, tiles(m), :]
                dve.wait_ge(root, m + 1)
                step(nc.vector.reciprocal(rec[:, tiles(m)], rec[:, tiles(m)]))
                nc.vector.tensor_tensor(part, part, over_columns(rec[:, tiles(m)], [P, NTN, F]),
                                        ALU.mult).then_inc(out_ready, 1)

            norm = (center, variance, scale)
            for c in range(CHUNKS):
                n = c % SLOTS
                dve.wait_ge(projected, c + 1)
                nc.vector.reciprocal(rden[:, n, :, :], ps[:, n, :, 2 * F:2 * F + 2]).then_inc(rden_step, 1)
                if c >= 1:
                    add_heads(c - 1)
                heads = ps[:, n, :, 0:2 * F].rearrange("p m (s c) -> p m s c", s=2)
                shape = [P, ITC * HP, 2, F]
                dve.wait_ge(rden_step, c + 1)
                if c >= SLOTS:
                    dve.wait_ge(y_read, c - SLOTS + 1)
                nc.vector.tensor_tensor(y[:, n, :, :, :].rearrange("p t (q s) c -> p (t q) s c", s=2), heads,
                                        rden[:, n, :, :].unsqueeze(3).to_broadcast(shape),
                                        ALU.mult).then_inc(divided, 1)
                m, stage = divmod(c - CHUNKS // NORMS, CHUNKS // NORMS)
                if m == 0 and stage < len(norm):
                    norm[stage](0)
            add_heads(CHUNKS - 1)
            for stage in norm:
                stage(NORMS - 1)

        @block.scalar
        def _(act):
            for m in range(NORMS):
                act.wait_ge(centered, m + 1)
                nc.scalar.activation(sq[:, tiles(m), :], o[:, tiles(m), :], ACT.Square).then_inc(squares, 1)
                act.wait_ge(var_ready, m + 1)
                nc.scalar.activation(rec[:, tiles(m)], var[:, tiles(m)], ACT.Sqrt).then_inc(root, 1)


def kernel(**inputs):
    import numpy as np
    import concourse.bacc as bacc
    from concourse.bass_utils import run_bass_kernel_spmd

    def laid(a):
        return np.ascontiguousarray(a)

    given = {name: np.asarray(a) for name, a in inputs.items()}
    x, adj, w0 = given["x"], given["adj"], given["L0_gnn_W"]
    arrays = {
        "x": laid(x), "xT": laid(x.T), "adj": laid(adj), "w0": laid(w0), "w0T": laid(w0.T),
        "a12": laid(given["L0_gnn_a"].reshape(2, F).T),
        "qwT": laid(given["L1_gnn_Qw"].T), "qb": laid(given["L1_gnn_Qb"]),
        "kwT": laid(given["L1_gnn_Kw"].T), "kb": laid(given["L1_gnn_Kb"]),
        "vwT": laid(given["L1_gnn_Vw"].T), "vb": laid(given["L1_gnn_Vb"]),
        "a_cat": laid(given["L1_gnn_a"].transpose(1, 0, 2).reshape(2 * D1, TYPES * H)),
        "pw": laid(given["L1_gnn_Pw"]), "pb": laid(given["L1_gnn_Pb"]),
    }
    nc = bacc.Bacc("TRN2", target_bir_lowering=False, num_devices=1)
    args = {name: nc.dram_tensor(f"in_{name}", a.shape, mybir.dt.from_np(a.dtype), kind="ExternalInput").ap()
            for name, a in arrays.items()}
    out = nc.dram_tensor("out_nodes", (N, F), F32, kind="ExternalOutput").ap()
    gat_program(nc, out=out, **args)
    result = run_bass_kernel_spmd(nc, [{f"in_{name}": a for name, a in arrays.items()}], core_ids=[0])
    return result.results[0]["out_nodes"]
```
